# Optimizing a Trainium2 kernel written in Bass

```python
import numpy as np
import jax
import jax.numpy as jnp

def _softmax(x, axis=-1):
    return jax.nn.softmax(x, axis=axis)

def _gelu(x):
    return jax.nn.gelu(x, approximate=True)

def _silu(x):
    return jax.nn.silu(x)

def _sigmoid(x):
    return jax.nn.sigmoid(x)

def _layernorm(x, axis=-1, eps=1e-05):
    m = jnp.mean(x, axis=axis, keepdims=True)
    v = jnp.var(x, axis=axis, keepdims=True)
    return (x - m) / jnp.sqrt(v + eps)

def _scatter_add(tgt, idx, src, axis=0):
    return tgt.at[idx].add(src)

def _segment_sum(src, seg, n):
    return jax.ops.segment_sum(src, seg, n)
kernel_name = 'mk_early_fusion_embed_d1_tok_img4096_r4_97c338'

def setup_inputs(seed: int=0):
    np.random.seed(seed)
    _w = jnp.asarray

    def _rec_inputs():
        import jax
        import jax.numpy as jnp
        _rk = jax.random.key(seed)
        x = -0.0043416 + 0.998921 * jax.random.normal(jax.random.fold_in(_rk, 1), (64, 64, 64, 2), jnp.float32)
        x_txt = jax.random.randint(jax.random.fold_in(_rk, 51), (64, 32), 0, 32027, jnp.int32)
        return (x, x_txt)
    x, x_txt = _rec_inputs()

    def _L0_tok_setup():
        import jax, jax.numpy as jnp
        import numpy as np
        H, N, CH = (64, 64, 1)
        key = jax.random.key(seed)
        k1, k2, k3 = jax.random.split(key, 3)
        A_abslog = jnp.log(jax.random.uniform(k1, (H, N), dtype=jnp.float32, minval=0.5, maxval=0.999))
        A_phase = jax.random.uniform(k2, (H, N), dtype=jnp.float32, minval=-np.pi, maxval=np.pi)
        C = jax.random.normal(k3, (CH, H, N, 2), dtype=jnp.float32)
        return {'A_abslog': A_abslog, 'A_phase': A_phase, 'C': C, 'L': 1024}
    _L0_tok_all = _L0_tok_setup()
    _L0_tok_in = {k: v for k, v in _L0_tok_all.items() if k in ('A_abslog', 'A_phase')}
    del _L0_tok_all

    def _L0_txt_setup():
        import jax, jax.numpy as jnp
        import numpy as np
        ORIG_VOCAB = 8000
        NEW_VOCAB = 32
        EMBED_DIM = 1024
        BATCH, SEQ = (4, 1024)
        key = jax.random.key(seed)
        k1, k2, k3 = jax.random.split(key, 3)
        input_ids = jax.random.randint(k1, (BATCH, SEQ), 0, ORIG_VOCAB + NEW_VOCAB, dtype=jnp.int64 if jax.config.jax_enable_x64 else jnp.int32)
        orig_table = jax.random.normal(k2, (ORIG_VOCAB, EMBED_DIM), dtype=jnp.float32) * 0.02
        new_table = jax.random.normal(k3, (NEW_VOCAB, EMBED_DIM), dtype=jnp.float32) * 0.02
        return {'input_ids': input_ids, 'orig_table': orig_table, 'new_table': new_table}
    _L0_txt_all = _L0_txt_setup()
    _L0_txt_in = {k: v for k, v in _L0_txt_all.items() if k in ('orig_table', 'new_table')}
    del _L0_txt_all

    def _L0_attn_setup():
        import jax, jax.numpy as jnp
        import numpy as np
        HIDDEN = 1024
        NUM_HEADS = 32
        HEAD_DIM = HIDDEN // NUM_HEADS

        def _fp8_roundtrip(x):
            return x.astype(jnp.float8_e4m3fn).astype(jnp.float32)
        key = jax.random.key(seed)
        ks = jax.random.split(key, 10)
        B, S = (2, 1024)
        hidden_states = jax.random.normal(ks[0], (B, S, HIDDEN), dtype=jnp.float32)
        scale = 0.02

        def lin(kw, kb):
            w = jax.random.normal(kw, (HIDDEN, HIDDEN), dtype=jnp.float32) * scale
            b = jax.random.normal(kb, (HIDDEN,), dtype=jnp.float32) * scale
            return (w, b)
        wq, bq = lin(ks[1], ks[2])
        wk, bk = lin(ks[3], ks[4])
        wv, bv = lin(ks[5], ks[6])
        wl, bl = lin(ks[7], ks[8])
        wq, bq = (_fp8_roundtrip(wq), _fp8_roundtrip(bq))
        wk, bk = (_fp8_roundtrip(wk), _fp8_roundtrip(bk))
        wv, bv = (_fp8_roundtrip(wv), _fp8_roundtrip(bv))
        return {'hidden_states': hidden_states, 'wq': wq, 'bq': bq, 'wk': wk, 'bk': bk, 'wv': wv, 'bv': bv, 'wl': wl, 'bl': bl}
    _L0_attn_all = _L0_attn_setup()
    _L0_attn_in = {k: v for k, v in _L0_attn_all.items() if k in ('wq', 'bq', 'wk', 'bk', 'wv', 'bv', 'wl', 'bl')}
    del _L0_attn_all

    def _L0_ffn_setup():
        import jax, jax.numpy as jnp
        import numpy as np
        E = 8
        R = 8
        DIN = 1024
        DOUT = 1024
        TOP_K = 2
        SCALING = 2.0

        def _moe_lora(xf, gate_W, A, B):
            gate_probs = jax.nn.softmax(xf @ gate_W.T, axis=-1)
            weights, sel = jax.lax.top_k(gate_probs, TOP_K)
            weights = weights / jnp.sum(weights, axis=-1, keepdims=True)
            T = xf.shape[0]
            w_dense = jnp.zeros((T, E), xf.dtype).at[jnp.arange(T)[:, None], sel].add(weights)
            h = jnp.einsum('td,erd->ter', xf, A)
            h = h * (w_dense[:, :, None] * SCALING)
            return jnp.einsum('ter,eor->to', h, B)
        key = jax.random.key(seed)
        k0, k1, k2, k3, k4 = jax.random.split(key, 5)
        x = jax.random.normal(k0, (4, 512, DIN), jnp.float32)
        W_base = jax.random.normal(k1, (DOUT, DIN), jnp.float32) * 0.02
        gate_W = jax.random.normal(k2, (E, DIN), jnp.float32) * 0.02
        A = jax.random.normal(k3, (E, R, DIN), jnp.float32) * 0.02
        B = jax.random.normal(k4, (E, DOUT, R), jnp.float32) * 0.02
        return {'x': x, 'W_base': W_base, 'gate_W': gate_W, 'A': A, 'B': B}
    _L0_ffn_all = _L0_ffn_setup()
    _L0_ffn_in = {k: v for k, v in _L0_ffn_all.items() if k in ('W_base', 'gate_W', 'A', 'B')}
    del _L0_ffn_all
    return {'x': x, 'x_txt': x_txt, 'L0_tok_A_abslog': _L0_tok_in['A_abslog'], 'L0_tok_A_phase': _L0_tok_in['A_phase'], 'L0_txt_orig_table': _L0_txt_in['orig_table'], 'L0_txt_new_table': _L0_txt_in['new_table'], 'L0_attn_wq': _L0_attn_in['wq'], 'L0_attn_bq': _L0_attn_in['bq'], 'L0_attn_wk': _L0_attn_in['wk'], 'L0_attn_bk': _L0_attn_in['bk'], 'L0_attn_wv': _L0_attn_in['wv'], 'L0_attn_bv': _L0_attn_in['bv'], 'L0_attn_wl': _L0_attn_in['wl'], 'L0_attn_bl': _L0_attn_in['bl'], 'L0_ffn_W_base': _L0_ffn_in['W_base'], 'L0_ffn_gate_W': _L0_ffn_in['gate_W'], 'L0_ffn_A': _L0_ffn_in['A'], 'L0_ffn_B': _L0_ffn_in['B']}

def reference(x, x_txt, L0_tok_A_abslog, L0_tok_A_phase, L0_txt_orig_table, L0_txt_new_table, L0_attn_wq, L0_attn_bq, L0_attn_wk, L0_attn_bk, L0_attn_wv, L0_attn_bv, L0_attn_wl, L0_attn_bl, L0_ffn_W_base, L0_ffn_gate_W, L0_ffn_A, L0_ffn_B):
    import jax
    import jax.numpy as jnp

    def _L0_tok_ref(A_abslog, A_phase, C, L):
        import jax, jax.numpy as jnp
        import numpy as np
        H, N, CH = (64, 64, 1)
        A = jnp.exp(A_abslog + 1j * A_phase)
        dtA = jnp.log(A)
        Cc = C[..., 0] + 1j * C[..., 1]
        Cc = Cc * (A - 1.0) / dtA
        t = jnp.arange(L, dtype=jnp.float32)
        K = jnp.exp(dtA[:, :, None] * t)
        K = jnp.einsum('chn,hnl->chl', Cc, K)
        return 2.0 * K.real

    def _L0_txt_ref(input_ids, orig_table, new_table):
        import jax, jax.numpy as jnp
        import numpy as np
        ORIG_VOCAB = 8000
        NEW_VOCAB = 32
        EMBED_DIM = 1024
        BATCH, SEQ = (4, 1024)
        is_new = input_ids >= ORIG_VOCAB
        orig_idx = jnp.where(is_new, 0, input_ids)
        new_idx = jnp.where(is_new, input_ids - ORIG_VOCAB, 0)
        orig_emb = orig_table[orig_idx]
        new_emb = new_table[new_idx]
        return jnp.where(is_new[..., None], new_emb, orig_emb)

    def _L0_attn_ref(hidden_states, wq, bq, wk, bk, wv, bv, wl, bl):
        import jax, jax.numpy as jnp
        import numpy as np
        HIDDEN = 1024
        NUM_HEADS = 32
        HEAD_DIM = HIDDEN // NUM_HEADS

        def _fp8_roundtrip(x):
            return x.astype(jnp.float8_e4m3fn).astype(jnp.float32)
        B, S, E = hidden_states.shape
        H, D = (NUM_HEADS, HEAD_DIM)
        q = (hidden_states @ wq.T + bq).reshape(B, S, H, D)
        k = (hidden_states @ wk.T + bk).reshape(B, S, H, D)
        v = (hidden_states @ wv.T + bv).reshape(B, S, H, D)
        latent = hidden_states @ wl.T + bl
        scores = jnp.einsum('bshd,bstd->bsht', q, k) / np.sqrt(D).astype(np.float32)
        probs = jax.nn.softmax(scores, axis=-1)
        context = jnp.einsum('bsht,bstd->bshd', probs, v).reshape(B, S, E)
        return context

    def _L0_ffn_ref(x, W_base, gate_W, A, B):
        import jax, jax.numpy as jnp
        import numpy as np
        E = 8
        R = 8
        DIN = 1024
        DOUT = 1024
        TOP_K = 2
        SCALING = 2.0

        def _moe_lora(xf, gate_W, A, B):
            gate_probs = jax.nn.softmax(xf @ gate_W.T, axis=-1)
            weights, sel = jax.lax.top_k(gate_probs, TOP_K)
            weights = weights / jnp.sum(weights, axis=-1, keepdims=True)
            T = xf.shape[0]
            w_dense = jnp.zeros((T, E), xf.dtype).at[jnp.arange(T)[:, None], sel].add(weights)
            h = jnp.einsum('td,erd->ter', xf, A)
            h = h * (w_dense[:, :, None] * SCALING)
            return jnp.einsum('ter,eor->to', h, B)
        xf = x.reshape(-1, x.shape[-1])
        out = xf @ W_base.T + _moe_lora(xf, gate_W, A, B)
        return out.reshape(*x.shape[:-1], DOUT)
    h = _L0_tok_ref(L0_tok_A_abslog, L0_tok_A_phase, x, 1024)
    h = jnp.concatenate([h, _L0_txt_ref(x_txt, L0_txt_orig_table, L0_txt_new_table)], axis=1)
    h = h + _L0_attn_ref(_layernorm(h, axis=-1), L0_attn_wq, L0_attn_bq, L0_attn_wk, L0_attn_bk, L0_attn_wv, L0_attn_bv, L0_attn_wl, L0_attn_bl)
    h = h + _L0_ffn_ref(_layernorm(h, axis=-1), L0_ffn_W_base, L0_ffn_gate_W, L0_ffn_A, L0_ffn_B)
    return h

_drawn_inputs = setup_inputs


def setup_inputs(seed=0):
    import zlib

    import numpy as np

    out = dict(_drawn_inputs(seed))
    spreads = {}
    factors = {'L0_attn_bq': 8.0, 'L0_attn_bk': 8.0, 'L0_attn_bv': 2.837}
    for name, (base, spread) in spreads.items():
        noise = np.random.default_rng([zlib.crc32(name.encode()), seed]).standard_normal(out[name].shape)
        drawn = base * np.exp(spread * noise) if base else spread * noise
        out[name] = jnp.asarray(drawn.astype(out[name].dtype))
    for name, factor in factors.items():
        out[name] = (out[name] * factor).astype(out[name].dtype)
    return out
```

```python
from contextlib import ExitStack

import concourse.bass as bass
from concourse import mybir

F32 = mybir.dt.float32
F16 = mybir.dt.float16
I32 = mybir.dt.int32
U32 = mybir.dt.uint32
ALU = mybir.AluOpType
ACT = mybir.ActivationFunctionType
AX = mybir.AxisListType

P = 128
D = 1024
KC = D // P
NHEAD = 32
HD = D // NHEAD
G = P // 32
TQ = P // G
HALF = 512
NE, RANK = 8, 8
NL = NE * RANK
NSSM = 64
NROW = 64
NCH = 64
NA, NB, NI = 16, 16, 4
NM = NA + NB + NI
TW = 2 * NA + 2 * NB + 2 * NI
NIT = 16
PIECES = 4
NTILE = 3 * NIT
VOCAB_OLD, VOCAB = 8000, 8032
EPS = 1e-5

X_SCALE = 2.0 ** 10
W_TOP = 14
QKV_DOWN = 2.0 ** -21
P_SCALE = 2.0 ** 14
EXP_MASK = 0x7F800000
INV_2PI = 0.15915494309189535
TWO_PI = 6.283185307179586
PI_BELOW = 3.1415925
C1 = 6.28125
C2 = TWO_PI - C1
ROUND = 1.5 * 2.0 ** 23
ROUND10 = 1.5 * 2.0 ** 13


def build_kernel(nc, craw, phase, abslog, consts, ids, table, wq, wk, wv, wb, bias, gate_a, lora_b, out):
    with ExitStack() as ctx:
        def sb(name, shape, dt):
            return ctx.enter_context(nc.sbuf_tensor(name, shape, dt))

        def sem(name):
            return ctx.enter_context(nc.semaphore(name))

        wsplit = {n: sb(f"w{n}_split", [P, 2, KC, D], F16) for n in "qkvb"}
        ga_split = sb("ga_split", [P, 2, KC, NE + NL], F16)
        lb_split = sb("lb_split", [P, 2, D], F16)
        const_sb = sb("const_sb", [P, NM + NE + P], F32)
        m_list = const_sb[:, 0:NM]
        iota8 = const_sb[:, NM:NM + NE]
        ident = const_sb[:, NM + NE:NM + NE + P]
        ident16 = sb("ident16", [P, P], F16)
        biasT = sb("biasT", [P, 3, 32], F32)
        idx_all = sb("idx_all", [P, NIT], U32)
        idx_now = sb("idx_now", [P, 1], U32)
        amax = sb("amax", [P, 10], F32)
        gmax = sb("gmax", [P, 10], F32)
        pow2 = sb("pow2", [P, 8], F32)
        up = sb("up", [P, 8], F32)
        down = sb("down", [P, 8], F32)
        fac = sb("fac", [P, 8], F32)
        neg_half = sb("neg_half", [P, 1], F32)
        stat = sb("stat", [P, 2, 12], F32)
        mv1 = sb("mv1", [P, 2], F32)
        mv2 = sb("mv2", [P, 2], F32)
        rs1 = sb("rs1", [P, 2], F32)
        rs2 = sb("rs2", [P, 2], F32)
        smax = sb("smax", [P, 32], F32)
        ssum = sb("ssum", [P, 32], F32)
        srec = sb("srec", [P, 32], F32)
        moe = sb("moe", [P, 96], F32)
        midx = sb("midx", [P, 8], U32)
        hsf = sb("hsf", [P, NL], F32)
        hs2 = sb("hs2", [P, 2, NL], F16)
        hsT = sb("hsT", [P, P], F16)

        region = sb("region", [P, 17296], F32)
        at = [0]

        def view(words):
            at[0] += words
            return region[:, at[0] - words:at[0]]

        h_buf = [view(D) for _ in range(3)]
        xn = view(D)
        x1T = view(D).bitcast(F16).rearrange("p (s k t) -> p s k t", s=2, k=KC)
        qT = view(D)
        kvT = view(D)
        s_mat = view(2 * NI * NCH)
        v_mat = view(2 * NA * NB)
        prod = view(2 * NA * NB)
        c_in = view(2 * 2 * NCH)
        tab_in = view(2 * TW)
        late = at[0]
        x2T = view(D).bitcast(F16).rearrange("p (s k t) -> p s k t", s=2, k=KC)
        diag_words = region[:, at[0]:at[0] + 4 * D]
        diag = view(4 * D).bitcast(F16).rearrange("p (s t m) -> p s t m", s=2, m=P)
        kT2 = view(D).bitcast(F16).rearrange("p (s e) -> p s e", s=2)
        prob = view(D)
        pT2 = prob.bitcast(F16).rearrange("p (s e) -> p s e", s=2)
        pT = view(D)
        assert at[0] == late + KC * D
        bw = wsplit["b"][:, :, :, :].rearrange("p s k n -> p (s k n)").bitcast(F32)
        stage = {"q": region[:, late:late + KC * D], "k": bw, "v": bw, "b": region[:, late:late + KC * D]}
        small_in = wsplit["k"][:, 1, :, :].rearrange("p k n -> p (k n)").bitcast(F32)
        ga_in = small_in[:, 0:KC * (NE + NL)]
        lb_in = small_in[:, 1024:2048]
        ph_in = small_in[:, 2048:2112]
        al_in = small_in[:, 2112:2176]
        id_in = small_in[:, 2176:2192].bitcast(I32)
        ph_w = small_in[:, 2200:2264]
        ph_h = small_in[:, 2264:2328]
        ph_l = small_in[:, 2328:2392]
        sm = [small_in[:, 2400 + 64 * i:2464 + 64 * i] for i in range(14)]
        idt = [small_in[:, 3400 + 16 * i:3416 + 16 * i] for i in range(2)]
        vw = wsplit["v"][:, :, :, :].rearrange("p s k n -> p (s k n)").bitcast(F32)
        ang, turn, low = (vw[:, 2304 * i:2304 * (i + 1)] for i in range(3))
        tab = region[:, 0:NROW * TW].rearrange("p (h w) -> p h w", w=TW)
        gtmp = [region[:, 4608 + 256 * i:4864 + 256 * i] for i in range(4)]
        tab_dram = nc.dram_tensor("power_tables", [P, NROW, TW], F32, kind="Internal").ap()

        pj = [ctx.enter_context(nc.psum_tensor(f"pj{i}", [P, HALF], F32)) for i in range(2)]
        ps_s = ctx.enter_context(nc.psum_tensor("ps_s", [P, D], F32))
        ps_c = ctx.enter_context(nc.psum_tensor("ps_c", [P, D], F32))
        ps_t = ctx.enter_context(nc.psum_tensor("ps_t", [P, D], F32))
        ps_g = ps_s[:, 0:NE + NL]
        ps_hs = ps_s[:, HALF:HALF + NL].bitcast(F16)

        names = """small_in const_in wq_in wk_in wv_in wb_in tab_out tab_in c_in gather row_out
        c_small c_idx c_ang c_cos c_exp c_re c_half c_tab c_g amax allmax scale whi wlo neg diag0 idnow
        sv_done tokgen_ps h_tok stat1 rstd1 xn1 x1t_ps x1_hi x1_lo
        proj evac biased k_hi k_lo dq_hi dq_lo dv_hi dv_lo
        scores smax_d ssub sexp ssum_d srec_d pnorm pT_d p_hi p_lo
        ctx_ps ctxT resid stat2 rstd2 xn2 x2t_ps x2_hi x2_lo
        gate_ps lg gexp held_v held_p moe_d hs_d hst_ps hst_sb ffn fev pool_c""".split()
        S = {n: sem("s_" + n) for n in names}
        block = ctx.enter_context(nc.Block())

        def three(v):
            return ((0, 0), (0, 1), (1, 0))

        @block.sync
        def _(sp):
            sp.dma_start(const_sb[:, :], consts).then_inc(S["const_in"], 16)
            for dst, src in ((ph_in, phase), (al_in, abslog), (id_in, ids), (biasT[:, :, :], bias), (ga_in, gate_a),
                             (lb_in, lora_b)):
                sp.dma_start(dst, src).then_inc(S["small_in"], 16)
            sp.dma_start(stage["q"], wq).then_inc(S["wq_in"], 16)
            sp.dma_start(stage["k"], wk).then_inc(S["wk_in"], 16)
            sp.wait_ge(S["c_tab"], 1)
            sp.dma_start(tab_dram, tab).then_inc(S["tab_out"], 16)
            sp.wait_ge(S["tab_out"], 16)

            def load_tok(q):
                sp.dma_start(tab_in.rearrange("p (h w) -> p h w", w=TW),
                             tab_dram[:, bass.ds(2 * q, 2), :]).then_inc(S["tab_in"], 16)
                sp.dma_start(c_in, craw[bass.ds(q, 1), :, :].rearrange("a p e -> p (a e)")).then_inc(S["c_in"], 16)

            load_tok(0)
            sp.wait_ge(S["wlo"], 1)
            sp.dma_start(stage["b"], wb).then_inc(S["wb_in"], 16)
            sp.wait_ge(S["sv_done"], 1)
            load_tok(1)
            sp.wait_ge(S["wlo"], 2)
            sp.dma_start(stage["v"], wv).then_inc(S["wv_in"], 16)

            def step(i, s, last):
                j = 3 * i + s
                sp.wait_ge(S["fev"], 2 * j)
                if not (isinstance(j, int) and j == 0):
                    store(j, s, i)
                if s < 2 and not last:
                    sp.wait_ge(S["sv_done"], 2 * i + s + 2)
                    load_tok(2 * i + s + 2)

            def store(j, s, i):
                sp.dma_start(out[bass.ds(P * (j - 1), P), :], h_buf[(s + 2) % 3]).then_inc(S["row_out"], 16)

            sp.wait_ge(S["sv_done"], 2)
            load_tok(2)
            step(0, 1, False)
            step(0, 2, False)
            with sp.Fori(1, NIT - 1) as i:
                for s in range(3):
                    step(i, s, False)
            for s in range(3):
                step(NIT - 1, s, True)
            sp.wait_ge(S["fev"], 2 * NTILE)
            sp.dma_start(out[P * (NTILE - 1):P * NTILE, :], h_buf[2]).then_inc(S["row_out"], 16)
            sp.wait_ge(S["row_out"], 16 * NTILE)

        @block.gpsimd
        def _(pool):
            g = nc.gpsimd
            g.memset(neg_half[:, :], -0.5).then_inc(S["neg"], 1)
            chain = [0]

            def all_max(n, a, b):
                pool.wait_ge(S["amax"], n)
                g.partition_all_reduce(gmax[:, a:b], amax[:, a:b], P, bass.bass_isa.ReduceOp.max)\
                    .then_inc(S["allmax"], 1)

            def sv_gen(q):
                cr, ci = (c_in[:, 2 * NCH * k:2 * NCH * (k + 1)].rearrange("p (h c) -> p h c", h=2)[:, :, None, :]
                          .broadcast_to([P, 2, NI, NCH]) for k in range(2))
                t = tab_in.rearrange("p (h w) -> p h w", w=TW)
                x1, x2 = (t[:, :, NA * k:NA * (k + 1)][:, :, :, None].broadcast_to([P, 2, NA, NB]) for k in range(2))
                y1, y2 = (t[:, :, 2 * NA + NB * k:2 * NA + NB * (k + 1)][:, :, None, :].broadcast_to([P, 2, NA, NB])
                          for k in range(2))
                o = 2 * NA + 2 * NB
                p1, p2 = (t[:, :, o + NI * k:o + NI * (k + 1)][:, :, :, None].broadcast_to([P, 2, NI, NCH])
                          for k in range(2))
                sm4 = s_mat.rearrange("p (h i c) -> p h i c", h=2, i=NI)
                pr4 = prod.rearrange("p (h i c) -> p h i c", h=2, i=NI)
                vm4 = v_mat.rearrange("p (h a b) -> p h a b", h=2, a=NA)
                pv4 = prod.rearrange("p (h a b) -> p h a b", h=2, a=NA)
                pool.wait_ge(S["tab_in"], 16 * (q + 1))
                pool.wait_ge(S["c_in"], 16 * (q + 1))
                pool.wait_ge(S["tokgen_ps"], q)
                g.tensor_tensor(out=sm4, in0=cr, in1=p1, op=ALU.mult)
                g.tensor_tensor(out=pr4, in0=ci, in1=p2, op=ALU.mult).then_inc(S["pool_c"], 1)
                pool.wait_ge(S["pool_c"], 3 * q + 1)
                g.tensor_tensor(out=s_mat, in0=s_mat, in1=prod, op=ALU.add)
                g.tensor_tensor(out=vm4, in0=x1, in1=y1, op=ALU.mult).then_inc(S["pool_c"], 1)
                pool.wait_ge(S["pool_c"], 3 * q + 2)
                g.tensor_tensor(out=pv4, in0=x2, in1=y2, op=ALU.mult).then_inc(S["pool_c"], 1)
                pool.wait_ge(S["pool_c"], 3 * q + 3)
                g.tensor_tensor(out=v_mat, in0=v_mat, in1=prod, op=ALU.add).then_inc(S["sv_done"], 1)

            def rstd(n, stat_sem, mv, rs, done):
                pool.wait_ge(S[stat_sem], 2 * n + 2)
                pool.sem_inc(S["held_p"], 1)
                g.tensor_scalar(rs[:, 0:1], mv[:, 1:2], X_SCALE ** -2, EPS * X_SCALE ** -2, ALU.mult, ALU.add)\
                    .then_inc(S[done], 1)
                pool.wait_ge(S[done], 2 * n + 1)
                g.tensor_tensor(out=rs[:, 1:2], in0=rs[:, 0:1], in1=neg_half[:, :], op=ALU.pow).then_inc(S[done], 1)

            pool.wait_ge(S["neg"], 1)
            all_max(1, 4, 10)
            all_max(2, 0, 1)
            all_max(3, 1, 2)
            sv_gen(0)
            rstd(0, "stat1", mv1, rs1, "rstd1")
            sv_gen(1)
            rstd(1, "stat1", mv1, rs1, "rstd1")
            all_max(4, 3, 4)
            all_max(5, 2, 3)
            pool.wait_ge(S["wlo"], 4)
            g.memset(diag_words, 0.0).then_inc(S["diag0"], 1)

            def step(i, s, last):
                j = 3 * i + s
                pool.wait_ge(S["srec_d"], j + 1)
                p3 = prob.rearrange("p (t g) -> p t g", g=32)
                g.tensor_tensor(out=p3, in0=p3, in1=srec[:, :, None].broadcast_to([P, 32, 32]), op=ALU.mult)\
                    .then_inc(S["pnorm"], 1)
                if s == 0:
                    pool.wait_ge(S["row_out"], 16 * j)
                    pool.wait_ge(S["gather"], 16 * i)
                    if isinstance(i, int) and i == 0:
                        pool.wait_ge(S["c_idx"], 3)
                    pool.sem_inc(S["held_p"], 1)
                    g.tensor_copy(idx_now[:, :], idx_all[:, bass.ds(i, 1)]).then_inc(S["idnow"], 1)
                    pool.wait_ge(S["idnow"], i + 1)
                    pool.sem_inc(S["held_p"], 1)
                    g.indirect_dma_start(h_buf[2], None, table,
                                         bass.IndirectOffsetOnAxis(ap=idx_now[:, :], axis=0),
                                         bounds_check=VOCAB - 1, oob_is_err=False).then_inc(S["gather"], 16)
                if s < 2 and not last:
                    sv_gen(2 * i + s + 2)
                if s == 0 or not last:
                    rstd(j + 2, "stat1", mv1, rs1, "rstd1")
                rstd(j, "stat2", mv2, rs2, "rstd2")

            for s in range(3):
                step(0, s, False)
            with pool.Fori(1, NIT - 1) as i:
                for s in range(3):
                    step(i, s, False)
            for s in range(3):
                step(NIT - 1, s, True)

        @block.vector
        def _(dve):
            v = nc.vector
            n_small = [0]

            def chained(ins, name):
                n_small[0] += 1
                ins.then_inc(S[name], 1)
                dve.wait_ge(S[name], n_small[0])

            dve.wait_ge(S["const_in"], 16)
            dve.wait_ge(S["small_in"], 16 * 6)
            v.tensor_copy(ident16[:, :], ident)
            for k in range(3):
                v.tensor_reduce(amax[:, 4 + k:5 + k], biasT[:, k, :], AX.X, ALU.max, apply_absolute_value=True)
            ga3 = ga_in.rearrange("p (k n) -> p k n", k=KC)
            v.tensor_reduce(amax[:, 7:8], ga3[:, :, 0:NE], AX.XY, ALU.max, apply_absolute_value=True)
            v.tensor_reduce(amax[:, 8:9], ga3[:, :, NE:], AX.XY, ALU.max, apply_absolute_value=True)
            v.tensor_reduce(amax[:, 9:10], lb_in, AX.X, ALU.max, apply_absolute_value=True).then_inc(S["amax"], 1)
            v.tensor_scalar(idt[0], id_in, 0.0, float(VOCAB_OLD), ALU.is_lt, ALU.mult).then_inc(S["c_idx"], 1)
            dve.wait_ge(S["c_idx"], 1)
            v.tensor_tensor(idt[1], id_in, idt[0], ALU.add).then_inc(S["c_idx"], 1)
            dve.wait_ge(S["c_idx"], 2)
            v.tensor_scalar(idx_all[:, :], idt[1], 0.0, float(VOCAB - 1), ALU.max, ALU.min).then_inc(S["c_idx"], 1)

            def abs_max(name):
                n = "qkvb".index(name)
                dve.wait_ge(S[f"w{name}_in"], 16)
                v.tensor_reduce(amax[:, n:n + 1], stage[name], AX.X, ALU.max, apply_absolute_value=True)\
                    .then_inc(S["amax"], 1)

            def link(ins):
                chained(ins, "c_small")

            link(v.tensor_scalar(sm[0], ph_in, INV_2PI, ROUND, ALU.mult, ALU.add))
            link(v.tensor_scalar(sm[0], sm[0], -ROUND, None, ALU.add))
            link(v.scalar_tensor_tensor(ph_w, sm[0], -C1, ph_in, ALU.mult, ALU.add))
            link(v.scalar_tensor_tensor(ph_w, sm[0], -C2, ph_w, ALU.mult, ALU.add))
            link(v.tensor_scalar(ph_h, ph_w, ROUND10, None, ALU.add))
            link(v.tensor_scalar(ph_h, ph_h, -ROUND10, None, ALU.add))
            link(v.tensor_tensor(ph_l, ph_w, ph_h, ALU.subtract))

            def hm(x):
                return x.rearrange("p (h m) -> p h m", m=NM)

            def per_h(x):
                return x[:, :, None].broadcast_to([P, NROW, NM])

            m_b = m_list[:, None, :].broadcast_to([P, NROW, NM])
            link(v.tensor_tensor(hm(ang), per_h(ph_h), m_b, ALU.mult))
            link(v.tensor_tensor(hm(low), per_h(ph_w), m_b, ALU.mult))
            link(v.tensor_scalar(turn, low, INV_2PI, ROUND, ALU.mult, ALU.add))
            link(v.tensor_scalar(turn, turn, -ROUND, None, ALU.add))
            link(v.scalar_tensor_tensor(ang, turn, -C1, ang, ALU.mult, ALU.add))
            link(v.tensor_tensor(hm(low), per_h(ph_l), m_b, ALU.mult))
            link(v.tensor_tensor(ang, ang, low, ALU.add))
            link(v.scalar_tensor_tensor(ang, turn, -C2, ang, ALU.mult, ALU.add))
            link(v.tensor_scalar(ang, ang, PI_BELOW, -PI_BELOW, ALU.min, ALU.max))
            link(v.tensor_scalar(turn, ang, 0.5 * 3.141592653589793, -TWO_PI, ALU.is_gt, ALU.mult))
            link(v.tensor_scalar(low, ang, 0.5 * 3.141592653589793, None, ALU.add))
            link(v.tensor_tensor(low, low, turn, ALU.add))
            link(v.tensor_scalar(low, low, PI_BELOW, -PI_BELOW, ALU.min, ALU.max))
            v.tensor_tensor(hm(turn), per_h(al_in), m_b, ALU.mult).then_inc(S["c_ang"], 1)
            abs_max("q")
            dve.wait_ge(S["c_exp"], 1)
            v.tensor_tensor(low, low, turn, ALU.mult)
            v.tensor_tensor(ang, ang, turn, ALU.mult).then_inc(S["c_re"], 1)
            dve.wait_ge(S["c_re"], 1)
            re, im = hm(low), hm(ang)
            link(v.tensor_scalar(sm[1], re[:, :, NA + 1], -1.0, None, ALU.add))
            link(v.tensor_copy(sm[2], im[:, :, NA + 1]))
            link(v.tensor_tensor(sm[3], al_in, al_in, ALU.mult))
            link(v.tensor_tensor(sm[4], ph_w, ph_w, ALU.mult))
            link(v.tensor_tensor(sm[3], sm[3], sm[4], ALU.add))
            link(v.reciprocal(sm[5], sm[3]))
            link(v.tensor_tensor(sm[6], sm[1], al_in, ALU.mult))
            link(v.tensor_tensor(sm[7], sm[2], ph_w, ALU.mult))
            link(v.tensor_tensor(sm[6], sm[6], sm[7], ALU.add))
            link(v.tensor_tensor(sm[8], sm[2], al_in, ALU.mult))
            link(v.tensor_tensor(sm[9], sm[1], ph_w, ALU.mult))
            link(v.tensor_tensor(sm[8], sm[8], sm[9], ALU.subtract))
            link(v.scalar_tensor_tensor(sm[10], sm[6], 2.0, sm[5], ALU.mult, ALU.mult))
            link(v.scalar_tensor_tensor(sm[11], sm[8], 2.0, sm[5], ALU.mult, ALU.mult))

            def hi4(x):
                return x.rearrange("p (h i) -> p h i", i=NI)

            wr, wi = (x[:, :, None].broadcast_to([P, NROW, NI]) for x in (sm[10], sm[11]))
            re_g, im_g = re[:, :, NA + NB:], im[:, :, NA + NB:]
            link(v.tensor_tensor(hi4(gtmp[0]), wr, re_g, ALU.mult))
            link(v.tensor_tensor(hi4(gtmp[1]), wi, im_g, ALU.mult))
            link(v.tensor_tensor(gtmp[0], gtmp[0], gtmp[1], ALU.subtract))
            link(v.tensor_tensor(hi4(gtmp[2]), wr, im_g, ALU.mult))
            link(v.tensor_tensor(hi4(gtmp[3]), wi, re_g, ALU.mult))
            v.tensor_tensor(gtmp[2], gtmp[2], gtmp[3], ALU.add).then_inc(S["c_g"], 1)

            def scale_of(k):
                pb, ub, db = (x[:, k:k + 1].bitcast(I32) for x in (pow2, up, down))
                link(v.tensor_scalar(pow2[:, k:k + 1], pow2[:, k:k + 1], 2.0 ** -40, None, ALU.max))
                link(v.tensor_scalar(pb, pb, EXP_MASK, None, ALU.bitwise_and))
                link(v.tensor_scalar(ub, pb, -1.0, float((2 * 127 + W_TOP) << 23), ALU.mult, ALU.add))
                link(v.tensor_scalar(db, pb, float(-(W_TOP << 23)), None, ALU.add))

            dve.wait_ge(S["allmax"], 1)
            for k, col in ((4, 7), (5, 8), (6, 9)):
                link(v.tensor_copy(pow2[:, k:k + 1], gmax[:, col:col + 1]))
                scale_of(k)
            lb_hi, lb_lo = lb_split[:, 0, :], lb_split[:, 1, :]
            for lo_c, hi_c, k in ((0, NE, 4), (NE, NE + NL, 5)):
                link(v.tensor_scalar(ga_split[:, 0, :, lo_c:hi_c], ga3[:, :, lo_c:hi_c], up[:, k:k + 1], None, ALU.mult))
                link(v.scalar_tensor_tensor(ga_split[:, 1, :, lo_c:hi_c], ga3[:, :, lo_c:hi_c], up[:, k:k + 1],
                                            ga_split[:, 0, :, lo_c:hi_c], ALU.mult, ALU.subtract))
            link(v.tensor_scalar(lb_hi, lb_in, up[:, 6:7], None, ALU.mult))
            link(v.scalar_tensor_tensor(lb_lo, lb_in, up[:, 6:7], lb_hi, ALU.mult, ALU.subtract))

            def norm_stats(n, slot, mv, w, sem_name):
                for k in range(2):
                    ins = v.bn_stats(stat[:, w, 6 * k:6 * k + 6], h_buf[slot][:, HALF * k:HALF * (k + 1)])
                ins.then_inc(S[sem_name], 1)
                dve.wait_ge(S[sem_name], 2 * n + 1)
                dve.sem_inc(S["held_v"], 1)
                v.bn_aggr(mv[:, :], stat[:, w, :]).then_inc(S[sem_name], 1)

            def norm_apply(n, slot, mv, rs, rsem, done):
                dve.wait_ge(S[rsem], 2 * n + 2)
                v.tensor_scalar(xn, h_buf[slot], mv[:, 0:1], rs[:, 1:2], ALU.subtract, ALU.mult).then_inc(S[done], 1)

            def split_lo(n, xT, hi_sem, lo_sem):
                dve.wait_ge(S[hi_sem], n + 1)
                v.tensor_tensor(xT[:, 1, :, :].rearrange("p k t -> p (k t)"), ps_t[:, :],
                                xT[:, 0, :, :].rearrange("p k t -> p (k t)"), ALU.subtract).then_inc(S[lo_sem], 1)

            def evac(n, u):
                dst = (qT, kvT, kvT)[u // 2].rearrange("p (t b) -> p b t", b=32)[:, 16 * (u % 2):16 * (u % 2) + 16, :]
                dve.wait_ge(S["proj"], 6 * n + u + 1)
                v.transpose(dst, pj[u % 2][:, :].rearrange("p (b t) -> p b t", t=32)).then_inc(S["evac"], 1)

            def add_bias(n, w):
                t3 = (qT, kvT, kvT)[w].rearrange("p (t b) -> p t b", b=32)
                dve.wait_ge(S["evac"], 6 * n + 2 * w + 2)
                v.scalar_tensor_tensor(t3, t3, QKV_DOWN, biasT[:, w, :][:, None, :].broadcast_to([P, 32, 32]),
                                       ALU.mult, ALU.add).then_inc(S["biased"], 1)

            def diag_lo(src, hi_sem, lo_sem, n, quadrants=range(G)):
                for r in quadrants:
                    q = slice(32 * r, 32 * r + 32)
                    dve.wait_ge(S[hi_sem], G * n + r + 1)
                    ins = v.tensor_tensor(diag[q, 1, :, q], src[q, :].rearrange("p (t b) -> p t b", b=32),
                                          diag[q, 0, :, q], ALU.subtract)
                if r == G - 1:
                    ins.then_inc(S[lo_sem], 1)

            def first_norm(n, slot, kind, q):
                if kind == "tok":
                    dve.wait_ge(S["h_tok"], q + 1)
                else:
                    dve.wait_ge(S["gather"], 16 * (q + 1))
                norm_stats(n, slot, mv1, 0, "stat1")

            def scale_weight(name, maxima):
                n = "qkvb".index(name)
                dve.wait_ge(S["allmax"], maxima)
                if n < 3:
                    link(v.scalar_tensor_tensor(pow2[:, n:n + 1], gmax[:, 4 + n:5 + n], 1.0 / 32, gmax[:, n:n + 1],
                                                ALU.mult, ALU.max))
                else:
                    link(v.tensor_tensor(fac[:, 7:8], pow2[:, 5:6], pow2[:, 6:7], ALU.mult))
                    link(v.scalar_tensor_tensor(pow2[:, n:n + 1], fac[:, 7:8], 128.0, gmax[:, n:n + 1],
                                                ALU.mult, ALU.max))
                scale_of(n)
                if n < 3:
                    ins = v.tensor_scalar(biasT[:, n, :], biasT[:, n, :], up[:, n:n + 1], X_SCALE * QKV_DOWN,
                                          ALU.mult, ALU.mult)
                else:
                    ins = v.tensor_scalar(fac[:, 5:6], down[:, 3:4], 1 / X_SCALE, None, ALU.mult)
                ins.then_inc(S["scale"], 1)

            def weight_lo(name):
                n = "qkvb".index(name)
                st3 = stage[name].rearrange("p (k n) -> p k n", k=KC)
                for c in range(PIECES):
                    ks = slice(c * KC // PIECES, (c + 1) * KC // PIECES)
                    dve.wait_ge(S["whi"], PIECES * n + c + 1)
                    lo = v.scalar_tensor_tensor(wsplit[name][:, 1, ks, :].rearrange("p k n -> p (k n)"),
                                                st3[:, ks, :].rearrange("p k n -> p (k n)"), up[:, n:n + 1],
                                                wsplit[name][:, 0, ks, :].rearrange("p k n -> p (k n)"),
                                                ALU.mult, ALU.subtract)
                lo.then_inc(S["wlo"], 1)

            scale_weight("q", 2)
            abs_max("k")
            weight_lo("q")
            scale_weight("k", 3)
            first_norm(0, 0, "tok", 0)
            norm_apply(0, 0, mv1, rs1, "rstd1", "xn1")
            split_lo(0, x1T, "x1_hi", "x1_lo")
            weight_lo("k")
            first_norm(1, 1, "tok", 1)
            evac(0, 0)
            abs_max("b")
            evac(0, 1)
            dve.wait_ge(S["scale"], 1)
            add_bias(0, 0)
            abs_max("v")
            scale_weight("v", 5)
            evac(0, 2)
            weight_lo("v")
            evac(0, 3)
            dve.wait_ge(S["scale"], 2)
            add_bias(0, 1)
            scale_weight("b", 5)
            back = 1.0 / (X_SCALE * QKV_DOWN)
            link(v.scalar_tensor_tensor(fac[:, 3:4], down[:, 0:1], back * back * HD ** -0.5, down[:, 1:2],
                                        ALU.mult, ALU.mult))
            link(v.tensor_scalar(fac[:, 4:5], down[:, 2:3], back / P_SCALE, None, ALU.mult))
            link(v.tensor_scalar(fac[:, 6:7], down[:, 4:5], 1 / X_SCALE, None, ALU.mult))
            link(v.scalar_tensor_tensor(fac[:, 7:8], down[:, 5:6], 2.0, up[:, 3:4], ALU.mult, ALU.mult))
            link(v.tensor_tensor(fac[:, 7:8], fac[:, 7:8], down[:, 6:7], ALU.mult))
            weight_lo("b")
            dve.wait_ge(S["k_hi"], 1)
            v.tensor_tensor(kT2[:, 1, :], kvT, kT2[:, 0, :], ALU.subtract).then_inc(S["k_lo"], 1)
            dve.wait_ge(S["diag0"], 1)
            diag_lo(qT, "dq_hi", "dq_lo", 0)
            dve.wait_ge(S["k_lo"], 1)
            for u in range(4, 6):
                evac(0, u)
            dve.wait_ge(S["scale"], 3)
            add_bias(0, 2)
            dve.wait_ge(S["x1t_ps"], 1)
            norm_apply(1, 1, mv1, rs1, "rstd1", "xn1")
            split_lo(1, x1T, "x1_hi", "x1_lo")

            def ffn_evac(n, slot):
                for k in range(2):
                    hs = h_buf[slot][:, HALF * k:HALF * (k + 1)]
                    dve.wait_ge(S["ffn"], 2 * n + k + 1)
                    v.scalar_tensor_tensor(hs, pj[k][:, :], fac[:, 5:6], hs, ALU.mult, ALU.add).then_inc(S["fev"], 1)

            def step(i, s, last):
                j = 3 * i + s
                more = not (last and s == 2)
                make = s == 0 or not last
                kind, q = (("text", i), ("tok", 2 * i + 2), ("tok", 2 * i + 3))[s]
                if not (isinstance(j, int) and j == 0):
                    ffn_evac(j - 1, (s + 2) % 3)
                sc3 = ps_s[:, :].rearrange("p (t g) -> p t g", g=32)
                p3 = prob.rearrange("p (t g) -> p t g", g=32)
                dve.wait_ge(S["scores"], j + 1)
                v.tensor_reduce(smax[:, :], sc3, AX.X, ALU.max).then_inc(S["smax_d"], 1)
                dve.wait_ge(S["smax_d"], j + 1)
                v.tensor_tensor(p3, sc3, smax[:, :, None].broadcast_to([P, 32, 32]), ALU.subtract).then_inc(S["ssub"], 1)
                dve.wait_ge(S["sexp"], j + 1)
                v.tensor_reduce(ssum[:, :], p3, AX.X, ALU.add).then_inc(S["ssum_d"], 1)
                dve.wait_ge(S["ssum_d"], 2 * j + 1)
                v.reciprocal(ssum[:, :], ssum[:, :]).then_inc(S["ssum_d"], 1)
                dve.wait_ge(S["ssum_d"], 2 * j + 2)
                v.tensor_scalar(srec[:, :], ssum[:, :], P_SCALE, None, ALU.mult).then_inc(S["srec_d"], 1)
                diag_lo(kvT, "dv_hi", "dv_lo", j, (0, 1))
                if more:
                    evac(j + 1, 0)
                diag_lo(kvT, "dv_hi", "dv_lo", j, (2, 3))
                dve.wait_ge(S["pnorm"], j + 1)
                v.transpose(pT, prob).then_inc(S["pT_d"], 1)
                dve.wait_ge(S["p_hi"], j + 1)
                v.tensor_tensor(pT2[:, 1, :], pT, pT2[:, 0, :], ALU.subtract).then_inc(S["p_lo"], 1)
                if more:
                    evac(j + 1, 1)
                    add_bias(j + 1, 0)
                if make:
                    first_norm(j + 2, (s + 2) % 3, kind, q)
                if more:
                    for u in (2, 3):
                        evac(j + 1, u)
                    add_bias(j + 1, 1)
                dve.wait_ge(S["ctx_ps"], j + 1)
                v.transpose(pT.rearrange("p (h d) -> p h d", d=32),
                            ps_c[:, :].rearrange("p (t h) -> p h t", h=32)).then_inc(S["ctxT"], 1)
                dve.wait_ge(S["ctxT"], j + 1)
                v.scalar_tensor_tensor(h_buf[s], pT, fac[:, 4:5], h_buf[s], ALU.mult, ALU.add).then_inc(S["resid"], 1)
                dve.wait_ge(S["resid"], j + 1)
                norm_stats(j, s, mv2, 1, "stat2")
                if more:
                    dve.wait_ge(S["k_hi"], j + 2)
                    v.tensor_tensor(kT2[:, 1, :], kvT, kT2[:, 0, :], ALU.subtract).then_inc(S["k_lo"], 1)
                if make or more:
                    dve.wait_ge(S["x1t_ps"], j + 2)
                norm_apply(j, s, mv2, rs2, "rstd2", "xn2")
                if more:
                    dve.wait_ge(S["k_lo"], j + 2)
                    evac(j + 1, 4)
                if make:
                    dve.wait_ge(S["x2t_ps"], j + 1)
                    norm_apply(j + 2, (s + 2) % 3, mv1, rs1, "rstd1", "xn1")
                split_lo(j, x2T, "x2_hi", "x2_lo")
                if more:
                    diag_lo(qT, "dq_hi", "dq_lo", j + 1)
                    evac(j + 1, 5)
                    add_bias(j + 1, 2)
                if make:
                    split_lo(j + 2, x1T, "x1_hi", "x1_lo")
                lg, e8, p8, t8 = (moe[:, 8 * k:8 * k + 8] for k in range(4))
                w0, w1 = moe[:, 32:40], moe[:, 40:48]
                nmx, sm1, rs_, d2, rd = (moe[:, 48 + k:49 + k] for k in range(5))
                ixf = moe[:, 56:58]
                base = 14 * j
                cnt = [0]

                def mchain(ins):
                    cnt[0] += 1
                    ins.then_inc(S["moe_d"], 1)
                    dve.wait_ge(S["moe_d"], base + cnt[0])

                dve.wait_ge(S["gate_ps"], j + 1)
                mchain(v.tensor_scalar(lg, ps_g[:, 0:NE], fac[:, 6:7], None, ALU.mult))
                v.tensor_reduce(nmx, lg, AX.X, ALU.max, negate=True).then_inc(S["lg"], 1)
                dve.wait_ge(S["gexp"], j + 1)
                mchain(v.reciprocal(rs_, sm1))
                mchain(v.tensor_scalar(p8, e8, rs_, None, ALU.mult))
                dve.sem_inc(S["held_v"], 1)
                mchain(v.max(t8, p8))
                dve.sem_inc(S["held_v"], 1)
                mchain(v.max_index(midx[:, :], t8, p8))
                mchain(v.tensor_copy(ixf, midx[:, 0:2]))
                mchain(v.tensor_tensor(d2, t8[:, 0:1], t8[:, 1:2], ALU.add))
                mchain(v.reciprocal(rd, d2))
                mchain(v.tensor_scalar(w0, iota8, ixf[:, 0:1], t8[:, 0:1], ALU.is_equal, ALU.mult))
                mchain(v.tensor_scalar(w1, iota8, ixf[:, 1:2], t8[:, 1:2], ALU.is_equal, ALU.mult))
                mchain(v.tensor_tensor(w0, w0, w1, ALU.add))
                mchain(v.tensor_scalar(w0, w0, rd, fac[:, 7:8], ALU.mult, ALU.mult))
                mchain(v.tensor_tensor(hsf[:, :].rearrange("p (e r) -> p e r", e=NE),
                                       ps_g[:, NE:NE + NL].rearrange("p (e r) -> p e r", e=NE),
                                       w0[:, :, None].broadcast_to([P, NE, RANK]), ALU.mult))
                mchain(v.tensor_copy(hs2[:, 0, :], hsf[:, :]))
                assert cnt[0] == 14
                v.tensor_tensor(hs2[:, 1, :], hsf[:, :], hs2[:, 0, :], ALU.subtract).then_inc(S["hs_d"], 1)

            for s in range(3):
                step(0, s, False)
            with dve.Fori(1, NIT - 1) as i:
                for s in range(3):
                    step(i, s, False)
            for s in range(3):
                step(NIT - 1, s, True)
            ffn_evac(NTILE - 1, 2)

        @block.scalar
        def _(act):
            a = nc.scalar

            act.wait_ge(S["c_ang"], 1)
            a.activation(ang, ang, ACT.Sin)
            a.activation(low, low, ACT.Sin)
            a.activation(turn, turn, ACT.Exp).then_inc(S["c_exp"], 1)
            act.wait_ge(S["c_re"], 1)
            lo_p, hi_p = slice(0, NSSM), slice(NSSM, P)
            re, im = (x.rearrange("p (h m) -> p h m", m=NM) for x in (low, ang))
            xa, yb = slice(0, NA), slice(NA, NA + NB)
            a.activation(tab[:, :, 0:NA], re[:, :, xa], ACT.Copy)
            a.activation(tab[lo_p, :, NA:2 * NA], im[lo_p, :, xa], ACT.Copy, scale=-1.0)
            a.activation(tab[hi_p, :, NA:2 * NA], im[hi_p, :, xa], ACT.Copy)
            o = 2 * NA
            a.activation(tab[lo_p, :, o:o + NB], re[lo_p, :, yb], ACT.Copy)
            a.activation(tab[hi_p, :, o:o + NB], im[hi_p, :, yb], ACT.Copy)
            a.activation(tab[lo_p, :, o + NB:o + 2 * NB], im[lo_p, :, yb], ACT.Copy)
            a.activation(tab[hi_p, :, o + NB:o + 2 * NB], re[hi_p, :, yb], ACT.Copy)
            o = 2 * NA + 2 * NB
            act.wait_ge(S["c_g"], 1)
            gre, gim = (gtmp[k].rearrange("p (h i) -> p h i", i=NI) for k in (0, 2))
            a.activation(tab[lo_p, :, o:o + NI], gre[lo_p, :, :], ACT.Copy)
            a.activation(tab[hi_p, :, o:o + NI], gim[hi_p, :, :], ACT.Copy, scale=-1.0)
            a.activation(tab[lo_p, :, o + NI:o + 2 * NI], gim[lo_p, :, :], ACT.Copy, scale=-1.0)
            a.activation(tab[hi_p, :, o + NI:o + 2 * NI], gre[hi_p, :, :], ACT.Copy, scale=-1.0).then_inc(S["c_tab"], 1)

            def weight_hi(name):
                n = "qkvb".index(name)
                st3 = stage[name].rearrange("p (k n) -> p k n", k=KC)
                act.wait_ge(S["scale"], n + 1)
                for c in range(PIECES):
                    ks = slice(c * KC // PIECES, (c + 1) * KC // PIECES)
                    a.activation(wsplit[name][:, 0, ks, :].rearrange("p k n -> p (k n)"),
                                 st3[:, ks, :].rearrange("p k n -> p (k n)"), ACT.Copy,
                                 scale=up[:, n:n + 1]).then_inc(S["whi"], 1)

            def h_evac(q, slot, j):
                act.wait_ge(S["tokgen_ps"], q + 1)
                if j is not None:
                    act.wait_ge(S["row_out"], 16 * j)
                a.activation(h_buf[slot], ps_t[:, :], ACT.Copy).then_inc(S["h_tok"], 1)

            def hi_of(n, xT, ready, done, before=None):
                act.wait_ge(S[ready], n + 1)
                if before is not None:
                    act.wait_ge(S["proj"], before)
                a.activation(xT[:, 0, :, :].rearrange("p k t -> p (k t)"), ps_t[:, :], ACT.Copy).then_inc(S[done], 1)

            def diag_hi(src, done):
                for r in range(G):
                    q = slice(32 * r, 32 * r + 32)
                    a.activation(diag[q, 0, :, q], src[q, :].rearrange("p (t b) -> p t b", b=32), ACT.Copy)\
                        .then_inc(S[done], 1)

            weight_hi("q")
            act.wait_ge(S["tab_out"], 16)
            h_evac(0, 0, None)
            hi_of(0, x1T, "x1t_ps", "x1_hi")
            weight_hi("k")
            h_evac(1, 1, None)
            weight_hi("v")
            act.wait_ge(S["wlo"], 3)
            weight_hi("b")
            act.wait_ge(S["wlo"], 4)
            act.wait_ge(S["biased"], 2)
            a.activation(kT2[:, 0, :], kvT, ACT.Copy).then_inc(S["k_hi"], 1)
            act.wait_ge(S["diag0"], 1)
            diag_hi(qT, "dq_hi")
            hi_of(1, x1T, "x1t_ps", "x1_hi", 6)

            def step(i, s, last):
                j = 3 * i + s
                more = not (last and s == 2)
                make = s == 0 or not last
                act.wait_ge(S["ssub"], j + 1)
                a.activation(prob, prob, ACT.Exp, scale=fac[:, 3:4]).then_inc(S["sexp"], 1)
                act.wait_ge(S["scores"], j + 1)
                act.wait_ge(S["biased"], 3 * j + 3)
                diag_hi(kvT, "dv_hi")
                if make and s > 0:
                    h_evac(2 * i + s + 1, (s + 2) % 3, j)
                act.wait_ge(S["pT_d"], j + 1)
                a.activation(pT2[:, 0, :], pT, ACT.Copy).then_inc(S["p_hi"], 1)
                if more:
                    act.wait_ge(S["biased"], 3 * j + 5)
                    a.activation(kT2[:, 0, :], kvT, ACT.Copy).then_inc(S["k_hi"], 1)
                hi_of(j, x2T, "x2t_ps", "x2_hi")
                if more:
                    act.wait_ge(S["ctx_ps"], j + 1)
                    act.wait_ge(S["biased"], 3 * j + 4)
                    diag_hi(qT, "dq_hi")
                if make:
                    hi_of(j + 2, x1T, "x1t_ps", "x1_hi", 6 * j + 12)
                act.wait_ge(S["lg"], j + 1)
                a.activation(moe[:, 8:16], moe[:, 0:8], ACT.Exp, bias=moe[:, 48:49], accum_out=moe[:, 49:50])\
                    .then_inc(S["gexp"], 1)
                act.wait_ge(S["hst_ps"], j + 1)
                a.activation(hsT[:, :], ps_hs, ACT.Copy).then_inc(S["hst_sb"], 1)

            for s in range(3):
                step(0, s, False)
            with act.Fori(1, NIT - 1) as i:
                for s in range(3):
                    step(i, s, False)
            for s in range(3):
                step(NIT - 1, s, True)

        @block.tensor
        def _(pe):
            t = nc.tensor
            PASSES = ((0, 0), (0, 1), (1, 0))

            def tokgen(q):
                pe.wait_ge(S["sv_done"], q + 1)
                for r in range(2):
                    for i4 in range(NI):
                        ins = t.matmul(ps_t[64 * r:64 * r + 64, 256 * i4:256 * i4 + 256],
                                       s_mat[:, (r * NI + i4) * NCH:(r * NI + i4 + 1) * NCH],
                                       v_mat[:, 256 * r:256 * r + 256], start=True, stop=True)
                ins.then_inc(S["tokgen_ps"], 1)

            def transposes(n, ready, done):
                pe.wait_ge(S[ready], n + 1)
                for k in range(KC):
                    ins = t.transpose(ps_t[:, P * k:P * (k + 1)], xn[:, P * k:P * (k + 1)], ident)
                ins.then_inc(S[done], 1)

            def unit(dst, xT, w, half, stop, chunks=range(KC)):
                for k in chunks:
                    for a, (x, y) in enumerate(PASSES):
                        ins = t.matmul(dst, xT[:, x, k, :], w[:, y, k, HALF * half:HALF * (half + 1)],
                                       start=(k == 0 and a == 0), stop=(stop and k == KC - 1 and a == 2))
                return ins

            V1_EARLY = 3

            def project(n, u, before=None, chunks=range(KC)):
                if u == 0:
                    pe.wait_ge(S["x1_lo"], n + 1)
                if u < 2:
                    if before is not None:
                        pe.wait_ge(S["fev"], before + u)
                else:
                    pe.wait_ge(S["evac"], 6 * n + u - 1)
                ins = unit(pj[u % 2][:, :], x1T, wsplit["qkv"[u // 2]], u % 2, True, chunks)
                if chunks[-1] == KC - 1:
                    ins.then_inc(S["proj"], 1)

            pe.wait_ge(S["const_in"], 16)
            tokgen(0)
            pe.wait_ge(S["h_tok"], 1)
            transposes(0, "xn1", "x1t_ps")
            pe.wait_ge(S["x1_lo"], 1)
            tokgen(1)
            for u in range(6):
                pe.wait_ge(S["wlo"], u // 2 + 1)
                project(0, u)
            pe.wait_ge(S["h_tok"], 2)
            transposes(1, "xn1", "x1t_ps")
            pe.wait_ge(S["wlo"], 4)

            def step(i, s, last):
                j = 3 * i + s
                first = isinstance(j, int) and j == 0
                more = not (last and s == 2)
                make = s == 0 or not last
                pe.wait_ge(S["dq_lo"], j + 1)
                pe.wait_ge(S["k_lo"], j + 1)
                if not first:
                    pe.wait_ge(S["hs_d"], j)
                    pe.wait_ge(S["hst_sb"], j)
                for tt in range(TQ):
                    for x, y in PASSES:
                        ins = t.matmul(ps_s[:, 32 * tt:32 * tt + 32], diag[:, x, tt, :], kT2[:, y, 32 * tt:32 * tt + 32],
                                       start=((x, y) == (0, 0)), stop=((x, y) == (1, 0)))
                ins.then_inc(S["scores"], 1)
                if more:
                    pe.wait_ge(S["x1_lo"], j + 2)
                if make and s > 0:
                    tokgen(2 * i + s + 1)
                if more:
                    for u in range(4):
                        project(j + 1, u, None if first else 2 * j - 1)
                pe.wait_ge(S["dv_lo"], j + 1)
                pe.wait_ge(S["p_lo"], j + 1)
                if not first:
                    pe.wait_ge(S["ctxT"], j)
                for tt in range(TQ):
                    for x, y in PASSES:
                        ins = t.matmul(ps_c[:, 32 * tt:32 * tt + 32], diag[:, x, tt, :], pT2[:, y, 32 * tt:32 * tt + 32],
                                       start=((x, y) == (0, 0)), stop=((x, y) == (1, 0)))
                ins.then_inc(S["ctx_ps"], 1)
                if more:
                    project(j + 1, 4)
                    project(j + 1, 5, chunks=range(V1_EARLY))
                if make and s > 0:
                    pe.wait_ge(S["h_tok"], 2 * i + s + 2)
                transposes(j, "xn2", "x2t_ps")
                if more:
                    project(j + 1, 5, chunks=range(V1_EARLY, KC))
                pe.wait_ge(S["x2_lo"], j + 1)
                if make:
                    transposes(j + 2, "xn1", "x1t_ps")
                pe.wait_ge(S["ssub"], j + 1)
                for k in range(KC):
                    for a, (x, y) in enumerate(PASSES):
                        ins = t.matmul(ps_g, x2T[:, x, k, :], ga_split[:, y, k, :],
                                       start=(k == 0 and a == 0), stop=(k == KC - 1 and a == 2))
                ins.then_inc(S["gate_ps"], 1)
                if more:
                    pe.wait_ge(S["evac"], 6 * j + 11)
                else:
                    pe.wait_ge(S["fev"], 2 * j - 1 + 0)
                unit(pj[0][:, :], x2T, wsplit["b"], 0, False)
                if more:
                    pe.wait_ge(S["evac"], 6 * j + 12)
                else:
                    pe.wait_ge(S["fev"], 2 * j)
                unit(pj[1][:, :], x2T, wsplit["b"], 1, False, range(KC - 1))
                pe.wait_ge(S["hs_d"], j + 1)
                t.transpose(ps_hs, hs2[:, :, :].rearrange("p s e -> p (s e)"), ident16[:, :]).then_inc(S["hst_ps"], 1)
                unit(pj[1][:, :], x2T, wsplit["b"], 1, False, range(KC - 1, KC))
                pe.wait_ge(S["hst_sb"], j + 1)
                for half in range(2):
                    for y in range(2):
                        ins = t.matmul(pj[half][:, :], hsT[:, :], lb_split[:, y, HALF * half:HALF * (half + 1)],
                                       start=False, stop=(y == 1))
                    ins.then_inc(S["ffn"], 1)

            for s in range(3):
                step(0, s, False)
            with pe.Fori(1, NIT - 1) as i:
                for s in range(3):
                    step(i, s, False)
            for s in range(3):
                step(NIT - 1, s, True)


def kernel(**inputs):
    import numpy as np
    import concourse.bacc as bacc
    from concourse import mybir as mb
    from concourse.bass_utils import run_bass_kernel_spmd

    def f(name):
        return np.asarray(inputs[name])

    def chunks(w):
        return w.T.reshape(KC, P, -1).transpose(1, 0, 2)

    def cat(*a):
        return np.concatenate(a, axis=0)

    x = f("x").transpose(3, 2, 1, 0)
    x = x.reshape(2, NSSM, NROW // 2, 2, NCH).transpose(2, 1, 0, 3, 4).reshape(NROW // 2, NSSM, -1)
    ph, al = f("L0_tok_A_phase").T, f("L0_tok_A_abslog").T
    wv = f("L0_attn_wv").reshape(NHEAD, HD, D).transpose(1, 0, 2).reshape(D, D)
    bq, bk = (f(n).reshape(NHEAD, HD).T for n in ("L0_attn_bq", "L0_attn_bk"))
    bv = f("L0_attn_bv").reshape(NHEAD, HD)
    bias = np.stack([cat(*[b] * G) for b in (bq, bk, bv)], axis=1)
    ga = chunks(cat(f("L0_ffn_gate_W"), f("L0_ffn_A").reshape(NL, D)))
    lb = f("L0_ffn_B").transpose(0, 2, 1).reshape(NL, D)
    consts = np.zeros((P, NM + NE + P), np.float32)
    consts[:, 0:NA] = 16 * np.arange(NA)
    consts[:, NA:NA + NB] = np.arange(NB)
    consts[:, NA + NB:NM] = 256 * np.arange(NI)
    consts[:, NM:NM + NE] = np.arange(NE)
    consts[:, NM + NE:] = np.eye(P)
    arrays = {
        "craw": np.concatenate([x, x], axis=1), "phase": cat(ph, ph), "abslog": cat(al, al), "consts": consts,
        "ids": f("x_txt").reshape(NIT, P).T,
        "table": cat(f("L0_txt_orig_table"), f("L0_txt_new_table")),
        "wq": chunks(f("L0_attn_wq")).reshape(P, -1), "wk": chunks(f("L0_attn_wk")).reshape(P, -1),
        "wv": chunks(wv).reshape(P, -1), "wb": chunks(f("L0_ffn_W_base")).reshape(P, -1),
        "bias": bias, "gate_a": ga.reshape(P, -1), "lora_b": cat(lb, lb),
    }
    arrays = {f"in_{k}": np.ascontiguousarray(v) for k, v in arrays.items()}
    nc = bacc.Bacc("TRN2", target_bir_lowering=False, num_devices=1)
    aps = [nc.dram_tensor(k, v.shape, mb.dt.from_np(v.dtype), kind="ExternalInput").ap() for k, v in arrays.items()]
    out = nc.dram_tensor("out_rows", (NTILE * P, D), mb.dt.float32, kind="ExternalOutput").ap()
    build_kernel(nc, *aps, out)
    rows = run_bass_kernel_spmd(nc, [arrays], core_ids=[0]).results[0]["out_rows"].reshape(NIT, 3, P, D)
    ssm = rows[:, 0:2].reshape(NROW, NCH, D).transpose(1, 0, 2)
    text = rows[:, 2].reshape(NCH, 32, D)
    return np.concatenate([ssm, text], axis=1)
```

```python
from contextlib import ExitStack

import concourse.bass as bass
from concourse import mybir

F32 = mybir.dt.float32
F16 = mybir.dt.float16
I32 = mybir.dt.int32
U32 = mybir.dt.uint32
ALU = mybir.AluOpType
ACT = mybir.ActivationFunctionType
AX = mybir.AxisListType

P = 128
D = 1024
KC = D // P
NHEAD = 32
HD = D // NHEAD
G = P // 32
TQ = P // G
HALF = 512
NE, RANK = 8, 8
NL = NE * RANK
NSSM = 64
NROW = 64
NCH = 64
NA, NB, NI = 16, 16, 4
NM = NA + NB + NI
TW = 2 * NA + 2 * NB + 2 * NI
NIT = 16
SHIFT = 2
NTILE = 3 * NIT
VOCAB_OLD, VOCAB = 8000, 8032
EPS = 1e-5

X_SCALE = 2.0 ** 10
W_TOP = 14
QKV_DOWN = 2.0 ** -21
P_SCALE = 2.0 ** 14
EXP_MASK = 0x7F800000
INV_2PI = 0.15915494309189535
TWO_PI = 6.283185307179586
PI_BELOW = 3.1415925
C1 = 6.28125
C2 = TWO_PI - C1
ROUND = 1.5 * 2.0 ** 23
ROUND10 = 1.5 * 2.0 ** 13


def build_kernel(nc, craw, phase, abslog, consts, ids, table, wq, wk, wv, wb, bias, gate_a, lora_b, out):
    with ExitStack() as ctx:
        def sb(name, shape, dt):
            return ctx.enter_context(nc.sbuf_tensor(name, shape, dt))

        def sem(name):
            return ctx.enter_context(nc.semaphore(name))

        ga_split = sb("ga_split", [P, 2, KC, NE + NL], F16)
        lb_split = sb("lb_split", [P, 2, D], F16)
        const_sb = sb("const_sb", [P, NM + NE + P], F32)
        m_list = const_sb[:, 0:NM]
        iota8 = const_sb[:, NM:NM + NE]
        ident = const_sb[:, NM + NE:NM + NE + P]
        ident16 = sb("ident16", [P, P], F16)
        biasT = sb("biasT", [P, 3, 32], F32)
        idx_all = sb("idx_all", [P, NIT], U32)
        idx_now = sb("idx_now", [P, 1], U32)
        ssq = sb("ssq", [P, 4, KC], F32)
        root = sb("root", [P, 4, KC], F32)
        amax = sb("amax", [P, 6], F32)
        gmax = sb("gmax", [P, 10], F32)
        pow2 = sb("pow2", [P, 8], F32)
        up = sb("up", [P, 8], F32)
        down = sb("down", [P, 8], F32)
        fac = sb("fac", [P, 8], F32)
        powers = sb("powers", [P, 3], F32)
        neg_half, plus_half, half_pi = (powers[:, k:k + 1] for k in range(3))
        stat = sb("stat", [P, 2, 12], F32)
        mv1 = sb("mv1", [P, 2], F32)
        mv2 = sb("mv2", [P, 2], F32)
        rs1 = sb("rs1", [P, 2], F32)
        rs2 = sb("rs2", [P, 2], F32)
        smax = sb("smax", [P, 32], F32)
        ssum = sb("ssum", [P, 32], F32)
        srec = sb("srec", [P, 32], F32)
        moe = sb("moe", [P, 96], F32)
        midx = sb("midx", [P, 8], U32)
        hsf = sb("hsf", [P, NL], F32)
        hs2 = sb("hs2", [P, 2, NL], F16)
        hsT = sb("hsT", [P, P], F16)

        area = sb("area", [P, 32 * D + 17296], F32)
        at = [0]

        def view(words):
            at[0] += words
            return area[:, at[0] - words:at[0]]

        weights = view(4 * KC * D)
        parts = weights.bitcast(F16).rearrange("p (n k s e) -> p n k s e", n=4, k=KC, s=2)
        wsplit = {n: parts[:, i] for i, n in enumerate("qkvb")}
        x2T = view(D).bitcast(F16).rearrange("p (s k t) -> p s k t", s=2, k=KC)
        pT = view(D)
        prob = view(D)
        pT2 = prob.bitcast(F16).rearrange("p (s e) -> p s e", s=2)
        kT2_words = view(D)
        kT2 = kT2_words.bitcast(F16).rearrange("p (s e) -> p s e", s=2)
        diag_words = view(4 * D)
        diag = diag_words.bitcast(F16).rearrange("p (s t m) -> p s t m", s=2, m=P)
        h1_at = at[0] + D
        h_buf = [view(D) for _ in range(3)]
        s_mat = view(2 * NI * NCH)
        v_mat = view(2 * NA * NB)
        prod = view(2 * NA * NB)
        c_in = view(2 * 2 * NCH)
        tab_in = view(2 * TW)
        xn = view(D)
        x1T = view(D).bitcast(F16).rearrange("p (s k t) -> p s k t", s=2, k=KC)
        qT = view(D)
        kvT = view(D)

        def stage(c, count=1):
            return area[:, (c + SHIFT) * D:(c + SHIFT + count) * D]

        ga_in, lb_in = diag_words[:, 0:KC * (NE + NL)], diag_words[:, 1024:2048]
        small = [diag_words[:, 2048 + 64 * i:2112 + 64 * i] for i in range(20)]
        ph_in, al_in, ph_w, ph_h, ph_l = small[0:5]
        sm = small[5:17]
        id_in = small[17][:, 0:16].bitcast(I32)
        idt = [small[17][:, 16 + 16 * i:32 + 16 * i] for i in range(2)]
        w_exp = [diag_words[:, 3328 + 256 * i:3584 + 256 * i] for i in range(2)]
        MH = NROW * NM
        assert NROW * TW == 2 * MH and 4 * MH <= (KC + 1) * D
        steps_at = (3 * KC + SHIFT) * D
        ang, cosv, turn, low = (area[:, steps_at + MH * i:steps_at + MH * (i + 1)] for i in range(4))
        tab = area[:, steps_at + 2 * MH:steps_at + 4 * MH].rearrange("p (h w) -> p h w", w=TW)
        expv = area[:, h1_at:h1_at + MH]
        gtmp = [kT2_words[:, 256 * i:256 * (i + 1)] for i in range(4)]
        tab_dram = nc.dram_tensor("power_tables", [P, NROW, TW], F32, kind="Internal").ap()

        pj = [ctx.enter_context(nc.psum_tensor(f"pj{i}", [P, HALF], F32)) for i in range(2)]
        ps_s = ctx.enter_context(nc.psum_tensor("ps_s", [P, D], F32))
        ps_c = ctx.enter_context(nc.psum_tensor("ps_c", [P, D], F32))
        ps_t = ctx.enter_context(nc.psum_tensor("ps_t", [P, D], F32))
        ps_g = ps_s[:, 0:NE + NL]
        ps_hs = ps_s[:, HALF:HALF + NL].bitcast(F16)

        names = """ids_in ph_in small_in const_in wq0_in wq1_in wk0_in wk1_in wv0_in wv1_in wb0_in wb1_in
        tab_out tab_in c_in gather row_out idnow
        c_small c_idx c_ph c_phm c_low c_am c_ang c_abs c_exp c_tab c_g
        amax allmax_small sumsq msq allmax scale whi wlo neg diag0
        sv_done tokgen_ps h_tok stat1 rstd1 xn1 x1t_ps x1_hi x1_lo
        proj evac biased k_hi k_lo dq_hi dq_lo dv_hi dv_lo
        scores smax_d ssub sexp ssum_d srec_d pnorm pT_d p_hi p_lo
        ctx_ps ctxT resid stat2 rstd2 xn2 x2t_ps x2_hi x2_lo
        gate_ps lg gexp held_v held_p moe_d hs_d hst_ps hst_sb ffn fev pool_c""".split()
        S = {n: sem("s_" + n) for n in names}
        block = ctx.enter_context(nc.Block())

        def load_weight(eng, name, src):
            c, half = KC * "qkvb".index(name), KC // 2
            for k in range(2):
                eng.dma_start(stage(c + half * k, half), src[:, half * D * k:half * D * (k + 1)])\
                    .then_inc(S[f"w{name}{k}_in"], 16)

        @block.sync
        def _(sp):
            sp.dma_start(id_in, ids).then_inc(S["ids_in"], 16)
            sp.dma_start(ph_in, phase).then_inc(S["ph_in"], 16)
            sp.dma_start(const_sb[:, :], consts).then_inc(S["const_in"], 16)
            for dst, src in ((al_in, abslog), (biasT[:, :, :], bias), (ga_in, gate_a), (lb_in, lora_b)):
                sp.dma_start(dst, src).then_inc(S["small_in"], 16)
            load_weight(sp, "q", wq)
            load_weight(sp, "k", wk)
            load_weight(sp, "v", wv)
            sp.wait_ge(S["c_tab"], 2)
            sp.dma_start(tab_dram, tab).then_inc(S["tab_out"], 16)
            sp.wait_ge(S["tab_out"], 16)

            def load_tok(q):
                sp.dma_start(tab_in.rearrange("p (h w) -> p h w", w=TW),
                             tab_dram[:, bass.ds(2 * q, 2), :]).then_inc(S["tab_in"], 16)
                sp.dma_start(c_in, craw[bass.ds(q, 1), :, :].rearrange("a p e -> p (a e)")).then_inc(S["c_in"], 16)

            load_tok(0)
            load_weight(sp, "b", wb)
            sp.wait_ge(S["sv_done"], 1)
            load_tok(1)

            def step(i, s, last):
                j = 3 * i + s
                if s != 1 and not last:
                    q = 2 * i + (2 if s == 0 else 3)
                    sp.wait_ge(S["sv_done"], q)
                    load_tok(q)
                if not (isinstance(j, int) and j == 0):
                    sp.wait_ge(S["fev"], 2 * j)
                    sp.dma_start(out[bass.ds(P * (j - 1), P), :], h_buf[(s + 2) % 3]).then_inc(S["row_out"], 16)

            for s in range(3):
                step(0, s, False)
            with sp.Fori(1, NIT - 1) as i:
                for s in range(3):
                    step(i, s, False)
            for s in range(3):
                step(NIT - 1, s, True)
            sp.wait_ge(S["fev"], 2 * NTILE)
            sp.dma_start(out[P * (NTILE - 1):P * NTILE, :], h_buf[2]).then_inc(S["row_out"], 16)
            sp.wait_ge(S["row_out"], 16 * NTILE)

        @block.gpsimd
        def _(pool):
            g = nc.gpsimd
            g.memset(neg_half, -0.5)
            g.memset(plus_half, 0.5)
            g.memset(half_pi, 0.5 * 3.141592653589793).then_inc(S["neg"], 1)

            def root_max(name):
                n = "qkvb".index(name)
                pool.wait_ge(S["sumsq"], KC * (n + 1))
                g.partition_all_reduce(root[:, n, :], ssq[:, n, :], P, bass.bass_isa.ReduceOp.max)\
                    .then_inc(S["msq"], 1)
                pool.wait_ge(S["msq"], n + 1)
                g.tensor_tensor(out=root[:, n, :], in0=root[:, n, :], in1=plus_half.broadcast_to([P, KC]), op=ALU.pow)\
                    .then_inc(S["allmax"], 1)

            def gather(i):
                pool.sem_inc(S["held_p"], 1)
                g.tensor_copy(idx_now[:, :], idx_all[:, bass.ds(i, 1)]).then_inc(S["idnow"], 1)
                pool.wait_ge(S["idnow"], i + 1)
                pool.sem_inc(S["held_p"], 1)
                g.indirect_dma_start(h_buf[0], None, table,
                                     bass.IndirectOffsetOnAxis(ap=idx_now[:, :], axis=0),
                                     bounds_check=VOCAB - 1, oob_is_err=False).then_inc(S["gather"], 16)

            def sv_gen(q):
                cr, ci = (c_in[:, 2 * NCH * k:2 * NCH * (k + 1)].rearrange("p (h c) -> p h c", h=2)[:, :, None, :]
                          .broadcast_to([P, 2, NI, NCH]) for k in range(2))
                t = tab_in.rearrange("p (h w) -> p h w", w=TW)
                x1, x2 = (t[:, :, NA * k:NA * (k + 1)][:, :, :, None].broadcast_to([P, 2, NA, NB]) for k in range(2))
                y1, y2 = (t[:, :, 2 * NA + NB * k:2 * NA + NB * (k + 1)][:, :, None, :].broadcast_to([P, 2, NA, NB])
                          for k in range(2))
                o = 2 * NA + 2 * NB
                p1, p2 = (t[:, :, o + NI * k:o + NI * (k + 1)][:, :, :, None].broadcast_to([P, 2, NI, NCH])
                          for k in range(2))
                sm4 = s_mat.rearrange("p (h i c) -> p h i c", h=2, i=NI)
                pr4 = prod.rearrange("p (h i c) -> p h i c", h=2, i=NI)
                vm4 = v_mat.rearrange("p (h a b) -> p h a b", h=2, a=NA)
                pv4 = prod.rearrange("p (h a b) -> p h a b", h=2, a=NA)
                pool.wait_ge(S["tab_in"], 16 * (q + 1))
                pool.wait_ge(S["c_in"], 16 * (q + 1))
                pool.wait_ge(S["tokgen_ps"], q)
                g.tensor_tensor(out=sm4, in0=cr, in1=p1, op=ALU.mult)
                g.tensor_tensor(out=pr4, in0=ci, in1=p2, op=ALU.mult).then_inc(S["pool_c"], 1)
                pool.wait_ge(S["pool_c"], 3 * q + 1)
                g.tensor_tensor(out=s_mat, in0=s_mat, in1=prod, op=ALU.add)
                g.tensor_tensor(out=vm4, in0=x1, in1=y1, op=ALU.mult).then_inc(S["pool_c"], 1)
                pool.wait_ge(S["pool_c"], 3 * q + 2)
                g.tensor_tensor(out=pv4, in0=x2, in1=y2, op=ALU.mult).then_inc(S["pool_c"], 1)
                pool.wait_ge(S["pool_c"], 3 * q + 3)
                g.tensor_tensor(out=v_mat, in0=v_mat, in1=prod, op=ALU.add).then_inc(S["sv_done"], 1)

            def rstd(n, stat_sem, mv, rs, done):
                pool.wait_ge(S[stat_sem], 2 * n + 2)
                pool.sem_inc(S["held_p"], 1)
                g.tensor_scalar(rs[:, 0:1], mv[:, 1:2], X_SCALE ** -2, EPS * X_SCALE ** -2, ALU.mult, ALU.add)\
                    .then_inc(S[done], 1)
                pool.wait_ge(S[done], 2 * n + 1)
                g.tensor_tensor(out=rs[:, 1:2], in0=rs[:, 0:1], in1=neg_half, op=ALU.pow).then_inc(S[done], 1)

            pool.wait_ge(S["neg"], 1)
            pool.wait_ge(S["c_idx"], 3)
            gather(0)

            def times_m(dst, src):
                return g.tensor_tensor(out=dst.rearrange("p (h m) -> p h m", m=NM),
                                       in0=src[:, :, None].broadcast_to([P, NROW, NM]),
                                       in1=m_list[:, None, :].broadcast_to([P, NROW, NM]), op=ALU.mult)

            pool.wait_ge(S["c_ph"], 1)
            pool.wait_ge(S["const_in"], 16)
            times_m(cosv, ph_w).then_inc(S["c_phm"], 1)
            times_m(low, ph_l).then_inc(S["c_low"], 1)
            pool.wait_ge(S["amax"], 1)
            g.partition_all_reduce(gmax[:, 4:10], amax[:, :], P, bass.bass_isa.ReduceOp.max).then_inc(S["allmax_small"], 1)
            root_max("q")
            rstd(0, "stat1", mv1, rs1, "rstd1")
            times_m(expv, al_in).then_inc(S["c_am"], 1)
            pool.wait_ge(S["c_exp"], 1)
            cos3, exp3 = (x.rearrange("p (h m) -> p h m", m=NM) for x in (cosv, expv))
            g.tensor_tensor(out=tab[:, :, 0:NA], in0=cos3[:, :, 0:NA], in1=exp3[:, :, 0:NA], op=ALU.mult)\
                .then_inc(S["c_tab"], 1)
            root_max("k")
            root_max("v")
            pool.wait_ge(S["c_g"], 1)
            g.memset(diag_words, 0.0).then_inc(S["diag0"], 1)
            sv_gen(0)
            rstd(1, "stat1", mv1, rs1, "rstd1")
            root_max("b")
            sv_gen(1)

            def step(i, s, last):
                j = 3 * i + s
                pool.wait_ge(S["srec_d"], j + 1)
                p3 = prob.rearrange("p (t g) -> p t g", g=32)
                g.tensor_tensor(out=p3, in0=p3, in1=srec[:, :, None].broadcast_to([P, 32, 32]), op=ALU.mult)\
                    .then_inc(S["pnorm"], 1)
                if s == 1 and not last:
                    pool.wait_ge(S["row_out"], 16 * j)
                    pool.wait_ge(S["gather"], 16 * i + 16)
                    gather(i + 1)
                if s == 0 and not last:
                    sv_gen(2 * i + 2)
                if s == 2 and not last:
                    sv_gen(2 * i + 3)
                if s == 0 or not last:
                    rstd(j + 2, "stat1", mv1, rs1, "rstd1")
                rstd(j, "stat2", mv2, rs2, "rstd2")

            for s in range(3):
                step(0, s, False)
            with pool.Fori(1, NIT - 1) as i:
                for s in range(3):
                    step(i, s, False)
            for s in range(3):
                step(NIT - 1, s, True)

        @block.vector
        def _(dve):
            v = nc.vector
            n_small = [0]

            def chained(ins, name):
                n_small[0] += 1
                ins.then_inc(S[name], 1)
                dve.wait_ge(S[name], n_small[0])

            dve.wait_ge(S["ids_in"], 16)
            v.tensor_scalar(idt[0], id_in, 0.0, float(VOCAB_OLD), ALU.is_lt, ALU.mult).then_inc(S["c_idx"], 1)
            dve.wait_ge(S["c_idx"], 1)
            v.tensor_tensor(idt[1], id_in, idt[0], ALU.add).then_inc(S["c_idx"], 1)
            dve.wait_ge(S["c_idx"], 2)
            v.tensor_scalar(idx_all[:, :], idt[1], 0.0, float(VOCAB - 1), ALU.max, ALU.min).then_inc(S["c_idx"], 1)
            dve.wait_ge(S["ph_in"], 16)

            def link(ins):
                chained(ins, "c_small")

            link(v.tensor_scalar(sm[0], ph_in, INV_2PI, ROUND, ALU.mult, ALU.add))
            link(v.tensor_scalar(sm[0], sm[0], -ROUND, None, ALU.add))
            link(v.scalar_tensor_tensor(ph_w, sm[0], -C1, ph_in, ALU.mult, ALU.add))
            link(v.scalar_tensor_tensor(ph_w, sm[0], -C2, ph_w, ALU.mult, ALU.add))
            link(v.tensor_scalar(ph_h, ph_w, ROUND10, None, ALU.add))
            link(v.tensor_scalar(ph_h, ph_h, -ROUND10, None, ALU.add))
            v.tensor_tensor(ph_l, ph_w, ph_h, ALU.subtract).then_inc(S["c_ph"], 1)
            dve.wait_ge(S["c_ph"], 1)

            def hm(x):
                return x.rearrange("p (h m) -> p h m", m=NM)

            def per_h(x):
                return x[:, :, None].broadcast_to([P, NROW, NM])

            def angles_a():
                m_b = m_list[:, None, :].broadcast_to([P, NROW, NM])
                link(v.tensor_tensor(hm(ang), per_h(ph_h), m_b, ALU.mult))
                dve.wait_ge(S["c_phm"], 1)
                link(v.tensor_scalar(turn, cosv, INV_2PI, ROUND, ALU.mult, ALU.add))
                link(v.tensor_scalar(turn, turn, -ROUND, None, ALU.add))
                link(v.scalar_tensor_tensor(ang, turn, -C1, ang, ALU.mult, ALU.add))

            def angles_b():
                dve.wait_ge(S["c_low"], 1)
                link(v.tensor_tensor(ang, ang, low, ALU.add))
                link(v.scalar_tensor_tensor(ang, turn, -C2, ang, ALU.mult, ALU.add))
                v.tensor_scalar(ang, ang, PI_BELOW, -PI_BELOW, ALU.min, ALU.max).then_inc(S["c_ang"], 1)

            def tables():
                dve.wait_ge(S["c_exp"], 1)
                cos3, sin3, exp3 = hm(cosv), hm(ang), hm(expv)
                lo_p, hi_p = slice(0, NSSM), slice(NSSM, P)
                xa, yb, ic, one = slice(0, NA), slice(NA, NA + NB), slice(NA + NB, NM), NA + 1
                link(v.tensor_tensor(sm[1], cos3[:, :, one], exp3[:, :, one], ALU.mult))
                link(v.tensor_scalar(sm[1], sm[1], -1.0, None, ALU.add))
                link(v.tensor_tensor(sm[2], sin3[:, :, one], exp3[:, :, one], ALU.mult))
                link(v.tensor_tensor(sm[3], al_in, al_in, ALU.mult))
                link(v.tensor_tensor(sm[4], ph_w, ph_w, ALU.mult))
                link(v.tensor_tensor(sm[3], sm[3], sm[4], ALU.add))
                link(v.reciprocal(sm[5], sm[3]))
                link(v.tensor_tensor(sm[6], sm[1], al_in, ALU.mult))
                link(v.tensor_tensor(sm[7], sm[2], ph_w, ALU.mult))
                link(v.tensor_tensor(sm[6], sm[6], sm[7], ALU.add))
                link(v.tensor_tensor(sm[8], sm[2], al_in, ALU.mult))
                link(v.tensor_tensor(sm[9], sm[1], ph_w, ALU.mult))
                link(v.tensor_tensor(sm[8], sm[8], sm[9], ALU.subtract))
                link(v.scalar_tensor_tensor(sm[10], sm[6], 2.0, sm[5], ALU.mult, ALU.mult))
                link(v.scalar_tensor_tensor(sm[11], sm[8], 2.0, sm[5], ALU.mult, ALU.mult))

                def hi4(x):
                    return x.rearrange("p (h i) -> p h i", i=NI)

                for k in range(2):
                    link(v.tensor_tensor(hi4(w_exp[k]), sm[10 + k][:, :, None].broadcast_to([P, NROW, NI]), exp3[:, :, ic],
                                         ALU.mult))
                link(v.tensor_tensor(hi4(gtmp[0]), hi4(w_exp[0]), cos3[:, :, ic], ALU.mult))
                link(v.tensor_tensor(hi4(gtmp[1]), hi4(w_exp[1]), sin3[:, :, ic], ALU.mult))
                link(v.tensor_tensor(hi4(gtmp[2]), hi4(w_exp[0]), sin3[:, :, ic], ALU.mult))
                link(v.tensor_tensor(hi4(gtmp[3]), hi4(w_exp[1]), cos3[:, :, ic], ALU.mult))
                g4 = [hi4(x) for x in gtmp]
                o = 2 * NA
                v.scalar_tensor_tensor(tab[lo_p, :, NA:2 * NA], sin3[lo_p, :, xa], -1.0, exp3[lo_p, :, xa], ALU.mult, ALU.mult)
                v.tensor_tensor(tab[hi_p, :, NA:2 * NA], sin3[hi_p, :, xa], exp3[hi_p, :, xa], ALU.mult)
                v.tensor_tensor(tab[lo_p, :, o:o + NB], cos3[lo_p, :, yb], exp3[lo_p, :, yb], ALU.mult)
                v.tensor_tensor(tab[hi_p, :, o:o + NB], sin3[hi_p, :, yb], exp3[hi_p, :, yb], ALU.mult)
                v.tensor_tensor(tab[lo_p, :, o + NB:o + 2 * NB], sin3[lo_p, :, yb], exp3[lo_p, :, yb], ALU.mult)
                v.tensor_tensor(tab[hi_p, :, o + NB:o + 2 * NB], cos3[hi_p, :, yb], exp3[hi_p, :, yb], ALU.mult)
                o = 2 * NA + 2 * NB
                p_c, q_c = slice(o, o + NI), slice(o + NI, o + 2 * NI)
                v.tensor_tensor(tab[lo_p, :, p_c], g4[0][lo_p], g4[1][lo_p], ALU.subtract)
                v.scalar_tensor_tensor(tab[hi_p, :, p_c], g4[2][hi_p], -1.0, g4[3][hi_p], ALU.mult, ALU.subtract)
                v.scalar_tensor_tensor(tab[lo_p, :, q_c], g4[2][lo_p], -1.0, g4[3][lo_p], ALU.mult, ALU.subtract)
                v.tensor_tensor(tab[hi_p, :, q_c], g4[1][hi_p], g4[0][hi_p], ALU.subtract).then_inc(S["c_tab"], 1)
                dve.wait_ge(S["c_tab"], 2)
                dve.sem_inc(S["c_g"], 1)

            def scale_of(k, count=1):
                cols = slice(k, k + count)
                pb, ub, db = (x[:, cols].bitcast(I32) for x in (pow2, up, down))
                link(v.tensor_scalar(pow2[:, cols], pow2[:, cols], 2.0 ** -40, None, ALU.max))
                link(v.tensor_scalar(pb, pb, EXP_MASK, None, ALU.bitwise_and))
                v.tensor_scalar(ub, pb, -1.0, float((2 * 127 + W_TOP) << 23), ALU.mult, ALU.add)
                link(v.tensor_scalar(db, pb, float(-(W_TOP << 23)), None, ALU.add))

            def norm_stats(n, slot, mv, w, sem_name):
                for k in range(2):
                    ins = v.bn_stats(stat[:, w, 6 * k:6 * k + 6], h_buf[slot][:, HALF * k:HALF * (k + 1)])
                ins.then_inc(S[sem_name], 1)
                dve.wait_ge(S[sem_name], 2 * n + 1)
                dve.sem_inc(S["held_v"], 1)
                v.bn_aggr(mv[:, :], stat[:, w, :]).then_inc(S[sem_name], 1)

            def norm_apply(n, slot, mv, rs, rsem, done):
                dve.wait_ge(S[rsem], 2 * n + 2)
                v.tensor_scalar(xn, h_buf[slot], mv[:, 0:1], rs[:, 1:2], ALU.subtract, ALU.mult).then_inc(S[done], 1)

            def split_lo(n, xT, hi_sem, lo_sem):
                dve.wait_ge(S[hi_sem], n + 1)
                v.tensor_tensor(xT[:, 1, :, :].rearrange("p k t -> p (k t)"), ps_t[:, :],
                                xT[:, 0, :, :].rearrange("p k t -> p (k t)"), ALU.subtract).then_inc(S[lo_sem], 1)

            def evac(n, u):
                dst = (qT, kvT, kvT)[u // 2].rearrange("p (t b) -> p b t", b=32)[:, 16 * (u % 2):16 * (u % 2) + 16, :]
                dve.wait_ge(S["proj"], 6 * n + u + 1)
                v.transpose(dst, pj[u % 2][:, :].rearrange("p (b t) -> p b t", t=32)).then_inc(S["evac"], 1)

            def add_bias(n, w):
                t3 = (qT, kvT, kvT)[w].rearrange("p (t b) -> p t b", b=32)
                dve.wait_ge(S["evac"], 6 * n + 2 * w + 2)
                v.scalar_tensor_tensor(t3, t3, QKV_DOWN, biasT[:, w, :][:, None, :].broadcast_to([P, 32, 32]),
                                       ALU.mult, ALU.add).then_inc(S["biased"], 1)

            def diag_lo(src, hi_sem, lo_sem, n, quadrants=range(G)):
                for r in quadrants:
                    q = slice(32 * r, 32 * r + 32)
                    dve.wait_ge(S[hi_sem], G * n + r + 1)
                    ins = v.tensor_tensor(diag[q, 1, :, q], src[q, :].rearrange("p (t b) -> p t b", b=32),
                                          diag[q, 0, :, q], ALU.subtract)
                if r == G - 1:
                    ins.then_inc(S[lo_sem], 1)

            def first_norm(n, slot, kind, q):
                if kind == "tok":
                    dve.wait_ge(S["h_tok"], q + 1)
                else:
                    dve.wait_ge(S["gather"], 16 * (q + 1))
                norm_stats(n, slot, mv1, 0, "stat1")

            ga3 = ga_in.rearrange("p (k n) -> p k n", k=KC)

            def magnitudes():
                for k in range(3):
                    v.tensor_reduce(amax[:, k:k + 1], biasT[:, k, :], AX.X, ALU.max, apply_absolute_value=True)
                v.tensor_reduce(amax[:, 3:4], ga3[:, :, 0:NE], AX.XY, ALU.max, apply_absolute_value=True)
                v.tensor_reduce(amax[:, 4:5], ga3[:, :, NE:], AX.XY, ALU.max, apply_absolute_value=True)
                v.tensor_reduce(amax[:, 5:6], lb_in, AX.X, ALU.max, apply_absolute_value=True).then_inc(S["amax"], 1)

            def expert_weights():
                dve.wait_ge(S["allmax_small"], 1)
                link(v.tensor_copy(pow2[:, 4:7], gmax[:, 7:10]))
                scale_of(4, 3)
                lb_hi, lb_lo = lb_split[:, 0, :], lb_split[:, 1, :]
                cols = ((slice(0, NE), 4), (slice(NE, NE + NL), 5))
                for c, k in cols:
                    v.tensor_scalar(ga_split[:, 0, :, c], ga3[:, :, c], up[:, k:k + 1], None, ALU.mult)
                link(v.tensor_scalar(lb_hi, lb_in, up[:, 6:7], None, ALU.mult))
                for c, k in cols:
                    v.scalar_tensor_tensor(ga_split[:, 1, :, c], ga3[:, :, c], up[:, k:k + 1], ga_split[:, 0, :, c],
                                           ALU.mult, ALU.subtract)
                link(v.scalar_tensor_tensor(lb_lo, lb_in, up[:, 6:7], lb_hi, ALU.mult, ALU.subtract))

            def scale_weight(name):
                n = "qkvb".index(name)
                dve.wait_ge(S["allmax"], n + 1)
                dve.wait_ge(S["allmax_small"], 1)
                link(v.tensor_reduce(gmax[:, n:n + 1], root[:, n, :], AX.X, ALU.max))
                if n < 3:
                    link(v.scalar_tensor_tensor(pow2[:, n:n + 1], gmax[:, 4 + n:5 + n], 1.0 / 32, gmax[:, n:n + 1],
                                                ALU.mult, ALU.max))
                else:
                    link(v.tensor_tensor(fac[:, 7:8], pow2[:, 5:6], pow2[:, 6:7], ALU.mult))
                    link(v.scalar_tensor_tensor(pow2[:, n:n + 1], fac[:, 7:8], 128.0, gmax[:, n:n + 1],
                                                ALU.mult, ALU.max))
                scale_of(n)
                if n < 3:
                    ins = v.tensor_scalar(biasT[:, n, :], biasT[:, n, :], up[:, n:n + 1], X_SCALE * QKV_DOWN,
                                          ALU.mult, ALU.mult)
                else:
                    ins = v.tensor_scalar(fac[:, 5:6], down[:, 3:4], 1 / X_SCALE, None, ALU.mult)
                ins.then_inc(S["scale"], 1)

            def weight_lo(name):
                n = "qkvb".index(name)
                for k in range(KC):
                    dve.wait_ge(S["whi"], KC * n + k + 1)
                    v.scalar_tensor_tensor(wsplit[name][:, k, 1, :], stage(KC * n + k), up[:, n:n + 1],
                                           wsplit[name][:, k, 0, :], ALU.mult, ALU.subtract).then_inc(S["wlo"], 1)

            dve.wait_ge(S["const_in"], 16)
            angles_a()
            v.tensor_copy(ident16[:, :], ident)
            dve.wait_ge(S["small_in"], 16 * 4)
            magnitudes()
            angles_b()
            first_norm(0, 0, "text", 0)
            scale_weight("q")
            norm_apply(0, 0, mv1, rs1, "rstd1", "xn1")
            weight_lo("q")
            split_lo(0, x1T, "x1_hi", "x1_lo")
            expert_weights()
            evac(0, 0)
            tables()
            scale_weight("k")
            weight_lo("k")
            scale_weight("v")
            evac(0, 1)
            dve.wait_ge(S["scale"], 1)
            add_bias(0, 0)
            weight_lo("v")
            evac(0, 2)
            evac(0, 3)
            dve.wait_ge(S["scale"], 2)
            add_bias(0, 1)
            dve.wait_ge(S["diag0"], 1)
            diag_lo(qT, "dq_hi", "dq_lo", 0)
            dve.wait_ge(S["k_hi"], 1)
            v.tensor_tensor(kT2[:, 1, :], kvT, kT2[:, 0, :], ALU.subtract).then_inc(S["k_lo"], 1)
            first_norm(1, 1, "tok", 0)
            dve.wait_ge(S["k_lo"], 1)
            evac(0, 4)
            dve.wait_ge(S["x1t_ps"], 1)
            norm_apply(1, 1, mv1, rs1, "rstd1", "xn1")
            evac(0, 5)
            dve.wait_ge(S["scale"], 3)
            add_bias(0, 2)
            split_lo(1, x1T, "x1_hi", "x1_lo")
            scale_weight("b")
            back = 1.0 / (X_SCALE * QKV_DOWN)
            link(v.scalar_tensor_tensor(fac[:, 3:4], down[:, 0:1], back * back * HD ** -0.5, down[:, 1:2],
                                        ALU.mult, ALU.mult))
            link(v.tensor_scalar(fac[:, 4:5], down[:, 2:3], back / P_SCALE, None, ALU.mult))
            link(v.tensor_scalar(fac[:, 6:7], down[:, 4:5], 1 / X_SCALE, None, ALU.mult))
            link(v.scalar_tensor_tensor(fac[:, 7:8], down[:, 5:6], 2.0, up[:, 3:4], ALU.mult, ALU.mult))
            link(v.tensor_tensor(fac[:, 7:8], fac[:, 7:8], down[:, 6:7], ALU.mult))
            weight_lo("b")

            def ffn_evac(n, slot):
                for k in range(2):
                    hs = h_buf[slot][:, HALF * k:HALF * (k + 1)]
                    dve.wait_ge(S["ffn"], 2 * n + k + 1)
                    v.scalar_tensor_tensor(hs, pj[k][:, :], fac[:, 5:6], hs, ALU.mult, ALU.add).then_inc(S["fev"], 1)

            def step(i, s, last):
                j = 3 * i + s
                more = not (last and s == 2)
                make = s == 0 or not last
                kind, q = (("tok", 2 * i + 1), ("text", i + 1), ("tok", 2 * i + 2))[s]
                if not (isinstance(j, int) and j == 0):
                    ffn_evac(j - 1, (s + 2) % 3)
                sc3 = ps_s[:, :].rearrange("p (t g) -> p t g", g=32)
                p3 = prob.rearrange("p (t g) -> p t g", g=32)
                dve.wait_ge(S["scores"], j + 1)
                v.tensor_reduce(smax[:, :], sc3, AX.X, ALU.max).then_inc(S["smax_d"], 1)
                dve.wait_ge(S["smax_d"], j + 1)
                v.tensor_tensor(p3, sc3, smax[:, :, None].broadcast_to([P, 32, 32]), ALU.subtract).then_inc(S["ssub"], 1)
                dve.wait_ge(S["sexp"], j + 1)
                v.tensor_reduce(ssum[:, :], p3, AX.X, ALU.add).then_inc(S["ssum_d"], 1)
                dve.wait_ge(S["ssum_d"], 2 * j + 1)
                v.reciprocal(ssum[:, :], ssum[:, :]).then_inc(S["ssum_d"], 1)
                dve.wait_ge(S["ssum_d"], 2 * j + 2)
                v.tensor_scalar(srec[:, :], ssum[:, :], P_SCALE, None, ALU.mult).then_inc(S["srec_d"], 1)
                diag_lo(kvT, "dv_hi", "dv_lo", j, (0, 1))
                if more:
                    evac(j + 1, 0)
                diag_lo(kvT, "dv_hi", "dv_lo", j, (2, 3))
                dve.wait_ge(S["pnorm"], j + 1)
                v.transpose(pT, prob).then_inc(S["pT_d"], 1)
                dve.wait_ge(S["p_hi"], j + 1)
                v.tensor_tensor(pT2[:, 1, :], pT, pT2[:, 0, :], ALU.subtract).then_inc(S["p_lo"], 1)
                if more:
                    evac(j + 1, 1)
                    add_bias(j + 1, 0)
                if make:
                    first_norm(j + 2, (s + 2) % 3, kind, q)
                if more:
                    for u in (2, 3):
                        evac(j + 1, u)
                    add_bias(j + 1, 1)
                dve.wait_ge(S["ctx_ps"], j + 1)
                v.transpose(pT.rearrange("p (h d) -> p h d", d=32),
                            ps_c[:, :].rearrange("p (t h) -> p h t", h=32)).then_inc(S["ctxT"], 1)
                dve.wait_ge(S["ctxT"], j + 1)
                v.scalar_tensor_tensor(h_buf[s], pT, fac[:, 4:5], h_buf[s], ALU.mult, ALU.add).then_inc(S["resid"], 1)
                dve.wait_ge(S["resid"], j + 1)
                norm_stats(j, s, mv2, 1, "stat2")
                if more:
                    dve.wait_ge(S["k_hi"], j + 2)
                    v.tensor_tensor(kT2[:, 1, :], kvT, kT2[:, 0, :], ALU.subtract).then_inc(S["k_lo"], 1)
                if make or more:
                    dve.wait_ge(S["x1t_ps"], j + 2)
                norm_apply(j, s, mv2, rs2, "rstd2", "xn2")
                if more:
                    dve.wait_ge(S["k_lo"], j + 2)
                    evac(j + 1, 4)
                if make:
                    dve.wait_ge(S["x2t_ps"], j + 1)
                    norm_apply(j + 2, (s + 2) % 3, mv1, rs1, "rstd1", "xn1")
                split_lo(j, x2T, "x2_hi", "x2_lo")
                if more:
                    diag_lo(qT, "dq_hi", "dq_lo", j + 1)
                    evac(j + 1, 5)
                    add_bias(j + 1, 2)
                if make:
                    split_lo(j + 2, x1T, "x1_hi", "x1_lo")
                lg, e8, p8, t8 = (moe[:, 8 * k:8 * k + 8] for k in range(4))
                w0, w1 = moe[:, 32:40], moe[:, 40:48]
                nmx, sm1, rs_, d2, rd = (moe[:, 48 + k:49 + k] for k in range(5))
                ixf = moe[:, 56:58]
                base = 14 * j
                cnt = [0]

                def mchain(ins):
                    cnt[0] += 1
                    ins.then_inc(S["moe_d"], 1)
                    dve.wait_ge(S["moe_d"], base + cnt[0])

                dve.wait_ge(S["gate_ps"], j + 1)
                mchain(v.tensor_scalar(lg, ps_g[:, 0:NE], fac[:, 6:7], None, ALU.mult))
                v.tensor_reduce(nmx, lg, AX.X, ALU.max, negate=True).then_inc(S["lg"], 1)
                dve.wait_ge(S["gexp"], j + 1)
                mchain(v.reciprocal(rs_, sm1))
                mchain(v.tensor_scalar(p8, e8, rs_, None, ALU.mult))
                dve.sem_inc(S["held_v"], 1)
                mchain(v.max(t8, p8))
                dve.sem_inc(S["held_v"], 1)
                mchain(v.max_index(midx[:, :], t8, p8))
                mchain(v.tensor_copy(ixf, midx[:, 0:2]))
                mchain(v.tensor_tensor(d2, t8[:, 0:1], t8[:, 1:2], ALU.add))
                mchain(v.reciprocal(rd, d2))
                mchain(v.tensor_scalar(w0, iota8, ixf[:, 0:1], t8[:, 0:1], ALU.is_equal, ALU.mult))
                mchain(v.tensor_scalar(w1, iota8, ixf[:, 1:2], t8[:, 1:2], ALU.is_equal, ALU.mult))
                mchain(v.tensor_tensor(w0, w0, w1, ALU.add))
                mchain(v.tensor_scalar(w0, w0, rd, fac[:, 7:8], ALU.mult, ALU.mult))
                mchain(v.tensor_tensor(hsf[:, :].rearrange("p (e r) -> p e r", e=NE),
                                       ps_g[:, NE:NE + NL].rearrange("p (e r) -> p e r", e=NE),
                                       w0[:, :, None].broadcast_to([P, NE, RANK]), ALU.mult))
                mchain(v.tensor_copy(hs2[:, 0, :], hsf[:, :]))
                assert cnt[0] == 14
                v.tensor_tensor(hs2[:, 1, :], hsf[:, :], hs2[:, 0, :], ALU.subtract).then_inc(S["hs_d"], 1)

            for s in range(3):
                step(0, s, False)
            with dve.Fori(1, NIT - 1) as i:
                for s in range(3):
                    step(i, s, False)
            for s in range(3):
                step(NIT - 1, s, True)
            ffn_evac(NTILE - 1, 2)

        @block.scalar
        def _(act):
            a = nc.scalar

            def sum_squares(name):
                n = "qkvb".index(name)
                for k in range(KC):
                    if k % (KC // 2) == 0:
                        act.wait_ge(S[f"w{name}{k // (KC // 2)}_in"], 16)
                    if n + k > 0:
                        act.wait_ge(S["sumsq"], KC * n + k)
                    a.activation(ps_c[:, :], stage(KC * n + k), ACT.Square,
                                 accum_out=ssq[:, n, k:k + 1]).then_inc(S["sumsq"], 1)

            def weight_hi(name):
                n = "qkvb".index(name)
                act.wait_ge(S["scale"], n + 1)
                for k in range(KC):
                    if KC * n + k >= SHIFT:
                        act.wait_ge(S["wlo"], KC * n + k - SHIFT + 1)
                    a.activation(wsplit[name][:, k, 0, :], stage(KC * n + k), ACT.Copy, scale=up[:, n:n + 1])\
                        .then_inc(S["whi"], 1)

            def h_evac(q, slot, j):
                act.wait_ge(S["tokgen_ps"], q + 1)
                if not (isinstance(j, int) and j == 0):
                    act.wait_ge(S["row_out"], 16 * j)
                a.activation(h_buf[slot], ps_t[:, :], ACT.Copy).then_inc(S["h_tok"], 1)

            def hi_of(n, xT, ready, done, before=None):
                act.wait_ge(S[ready], n + 1)
                if before is not None:
                    act.wait_ge(S["proj"], before)
                a.activation(xT[:, 0, :, :].rearrange("p k t -> p (k t)"), ps_t[:, :], ACT.Copy).then_inc(S[done], 1)

            def diag_hi(src, done):
                for r in range(G):
                    q = slice(32 * r, 32 * r + 32)
                    a.activation(diag[q, 0, :, q], src[q, :].rearrange("p (t b) -> p t b", b=32), ACT.Copy)\
                        .then_inc(S[done], 1)

            sum_squares("q")
            weight_hi("q")
            hi_of(0, x1T, "x1t_ps", "x1_hi")
            act.wait_ge(S["neg"], 1)
            act.wait_ge(S["c_ang"], 1)
            a.activation(cosv, ang, ACT.Abs).then_inc(S["c_abs"], 1)
            act.wait_ge(S["c_abs"], 1)
            a.activation(cosv, cosv, ACT.Sin, scale=-1.0, bias=half_pi)
            a.activation(ang, ang, ACT.Sin)
            act.wait_ge(S["c_am"], 1)
            a.activation(expv, expv, ACT.Exp).then_inc(S["c_exp"], 1)
            sum_squares("k")
            sum_squares("v")
            weight_hi("k")
            weight_hi("v")
            act.wait_ge(S["diag0"], 1)
            act.wait_ge(S["biased"], 1)
            diag_hi(qT, "dq_hi")
            act.wait_ge(S["biased"], 2)
            a.activation(kT2[:, 0, :], kvT, ACT.Copy).then_inc(S["k_hi"], 1)
            h_evac(0, 1, 0)
            sum_squares("b")
            hi_of(1, x1T, "x1t_ps", "x1_hi", 6)
            weight_hi("b")

            def step(i, s, last):
                j = 3 * i + s
                more = not (last and s == 2)
                make = s == 0 or not last
                act.wait_ge(S["ssub"], j + 1)
                a.activation(prob, prob, ACT.Exp, scale=fac[:, 3:4]).then_inc(S["sexp"], 1)
                act.wait_ge(S["scores"], j + 1)
                act.wait_ge(S["biased"], 3 * j + 3)
                diag_hi(kvT, "dv_hi")
                if make and s != 1:
                    h_evac(2 * i + 1 + s // 2, (s + 2) % 3, j)
                act.wait_ge(S["pT_d"], j + 1)
                a.activation(pT2[:, 0, :], pT, ACT.Copy).then_inc(S["p_hi"], 1)
                if more:
                    act.wait_ge(S["biased"], 3 * j + 5)
                    a.activation(kT2[:, 0, :], kvT, ACT.Copy).then_inc(S["k_hi"], 1)
                hi_of(j, x2T, "x2t_ps", "x2_hi")
                if more:
                    act.wait_ge(S["ctx_ps"], j + 1)
                    act.wait_ge(S["biased"], 3 * j + 4)
                    diag_hi(qT, "dq_hi")
                if make:
                    hi_of(j + 2, x1T, "x1t_ps", "x1_hi", 6 * j + 12)
                act.wait_ge(S["lg"], j + 1)
                a.activation(moe[:, 8:16], moe[:, 0:8], ACT.Exp, bias=moe[:, 48:49], accum_out=moe[:, 49:50])\
                    .then_inc(S["gexp"], 1)
                act.wait_ge(S["hst_ps"], j + 1)
                a.activation(hsT[:, :], ps_hs, ACT.Copy).then_inc(S["hst_sb"], 1)

            for s in range(3):
                step(0, s, False)
            with act.Fori(1, NIT - 1) as i:
                for s in range(3):
                    step(i, s, False)
            for s in range(3):
                step(NIT - 1, s, True)

        @block.tensor
        def _(pe):
            t = nc.tensor
            PASSES = ((0, 0), (0, 1), (1, 0))

            def tokgen(q):
                pe.wait_ge(S["sv_done"], q + 1)
                for r in range(2):
                    for i4 in range(NI):
                        ins = t.matmul(ps_t[64 * r:64 * r + 64, 256 * i4:256 * i4 + 256],
                                       s_mat[:, (r * NI + i4) * NCH:(r * NI + i4 + 1) * NCH],
                                       v_mat[:, 256 * r:256 * r + 256], start=True, stop=True)
                ins.then_inc(S["tokgen_ps"], 1)

            def transposes(n, ready, done):
                pe.wait_ge(S[ready], n + 1)
                for k in range(KC):
                    ins = t.transpose(ps_t[:, P * k:P * (k + 1)], xn[:, P * k:P * (k + 1)], ident)
                ins.then_inc(S[done], 1)

            def unit(dst, xT, w, half, stop, chunks=range(KC)):
                for k in chunks:
                    for a, (x, y) in enumerate(PASSES):
                        ins = t.matmul(dst, xT[:, x, k, :], w[:, k, y, HALF * half:HALF * (half + 1)],
                                       start=(k == 0 and a == 0), stop=(stop and k == KC - 1 and a == 2))
                return ins

            V1_EARLY = 3

            def project(n, u, before=None, chunks=range(KC)):
                if u == 0:
                    pe.wait_ge(S["x1_lo"], n + 1)
                if u < 2:
                    if before is not None:
                        pe.wait_ge(S["fev"], before + u)
                else:
                    pe.wait_ge(S["evac"], 6 * n + u - 1)
                ins = unit(pj[u % 2][:, :], x1T, wsplit["qkv"[u // 2]], u % 2, True, chunks)
                if chunks[-1] == KC - 1:
                    ins.then_inc(S["proj"], 1)

            pe.wait_ge(S["const_in"], 16)
            transposes(0, "xn1", "x1t_ps")
            for u in range(6):
                if u == 4:
                    tokgen(0)
                for k in range(KC):
                    pe.wait_ge(S["wlo"], KC * (u // 2) + k + 1)
                    project(0, u, chunks=range(k, k + 1))
            pe.wait_ge(S["h_tok"], 1)
            transposes(1, "xn1", "x1t_ps")

            def step(i, s, last):
                j = 3 * i + s
                first = isinstance(j, int) and j == 0
                more = not (last and s == 2)
                make = s == 0 or not last
                pe.wait_ge(S["dq_lo"], j + 1)
                pe.wait_ge(S["k_lo"], j + 1)
                if not first:
                    pe.wait_ge(S["hs_d"], j)
                    pe.wait_ge(S["hst_sb"], j)
                for tt in range(TQ):
                    for x, y in PASSES:
                        ins = t.matmul(ps_s[:, 32 * tt:32 * tt + 32], diag[:, x, tt, :], kT2[:, y, 32 * tt:32 * tt + 32],
                                       start=((x, y) == (0, 0)), stop=((x, y) == (1, 0)))
                ins.then_inc(S["scores"], 1)
                if more:
                    pe.wait_ge(S["x1_lo"], j + 2)
                if make and s != 1:
                    tokgen(2 * i + 1 + s // 2)
                if more:
                    for u in range(4):
                        project(j + 1, u, None if first else 2 * j - 1)
                pe.wait_ge(S["dv_lo"], j + 1)
                pe.wait_ge(S["p_lo"], j + 1)
                if not first:
                    pe.wait_ge(S["ctxT"], j)
                for tt in range(TQ):
                    for x, y in PASSES:
                        ins = t.matmul(ps_c[:, 32 * tt:32 * tt + 32], diag[:, x, tt, :], pT2[:, y, 32 * tt:32 * tt + 32],
                                       start=((x, y) == (0, 0)), stop=((x, y) == (1, 0)))
                ins.then_inc(S["ctx_ps"], 1)
                if more:
                    project(j + 1, 4)
                    project(j + 1, 5, chunks=range(V1_EARLY))
                if make and s != 1:
                    pe.wait_ge(S["h_tok"], 2 * i + 2 + s // 2)
                transposes(j, "xn2", "x2t_ps")
                if more:
                    project(j + 1, 5, chunks=range(V1_EARLY, KC))
                pe.wait_ge(S["x2_lo"], j + 1)
                if make:
                    transposes(j + 2, "xn1", "x1t_ps")
                pe.wait_ge(S["ssub"], j + 1)
                for k in range(KC):
                    for a, (x, y) in enumerate(PASSES):
                        ins = t.matmul(ps_g, x2T[:, x, k, :], ga_split[:, y, k, :],
                                       start=(k == 0 and a == 0), stop=(k == KC - 1 and a == 2))
                ins.then_inc(S["gate_ps"], 1)
                if more:
                    pe.wait_ge(S["evac"], 6 * j + 11)
                else:
                    pe.wait_ge(S["fev"], 2 * j - 1)
                if first:
                    pe.wait_ge(S["wlo"], 4 * KC)
                unit(pj[0][:, :], x2T, wsplit["b"], 0, False)
                if more:
                    pe.wait_ge(S["evac"], 6 * j + 12)
                else:
                    pe.wait_ge(S["fev"], 2 * j)
                unit(pj[1][:, :], x2T, wsplit["b"], 1, False, range(KC - 1))
                pe.wait_ge(S["hs_d"], j + 1)
                t.transpose(ps_hs, hs2[:, :, :].rearrange("p s e -> p (s e)"), ident16[:, :]).then_inc(S["hst_ps"], 1)
                unit(pj[1][:, :], x2T, wsplit["b"], 1, False, range(KC - 1, KC))
                pe.wait_ge(S["hst_sb"], j + 1)
                for half in range(2):
                    for y in range(2):
                        ins = t.matmul(pj[half][:, :], hsT[:, :], lb_split[:, y, HALF * half:HALF * (half + 1)],
                                       start=False, stop=(y == 1))
                    ins.then_inc(S["ffn"], 1)

            for s in range(3):
                step(0, s, False)
            with pe.Fori(1, NIT - 1) as i:
                for s in range(3):
                    step(i, s, False)
            for s in range(3):
                step(NIT - 1, s, True)


def kernel(**inputs):
    import numpy as np
    import concourse.bacc as bacc
    from concourse import mybir as mb
    from concourse.bass_utils import run_bass_kernel_spmd

    def f(name):
        return np.asarray(inputs[name])

    def chunks(w):
        return w.T.reshape(KC, P, -1).transpose(1, 0, 2)

    def cat(*a):
        return np.concatenate(a, axis=0)

    x = f("x").transpose(3, 2, 1, 0)
    x = x.reshape(2, NSSM, NROW // 2, 2, NCH).transpose(2, 1, 0, 3, 4).reshape(NROW // 2, NSSM, -1)
    ph, al = f("L0_tok_A_phase").T, f("L0_tok_A_abslog").T
    wv = f("L0_attn_wv").reshape(NHEAD, HD, D).transpose(1, 0, 2).reshape(D, D)
    bq, bk = (f(n).reshape(NHEAD, HD).T for n in ("L0_attn_bq", "L0_attn_bk"))
    bv = f("L0_attn_bv").reshape(NHEAD, HD)
    bias = np.stack([cat(*[b] * G) for b in (bq, bk, bv)], axis=1)
    ga = chunks(cat(f("L0_ffn_gate_W"), f("L0_ffn_A").reshape(NL, D)))
    lb = f("L0_ffn_B").transpose(0, 2, 1).reshape(NL, D)
    consts = np.zeros((P, NM + NE + P), np.float32)
    consts[:, 0:NA] = 16 * np.arange(NA)
    consts[:, NA:NA + NB] = np.arange(NB)
    consts[:, NA + NB:NM] = 256 * np.arange(NI)
    consts[:, NM:NM + NE] = np.arange(NE)
    consts[:, NM + NE:] = np.eye(P)
    arrays = {
        "craw": np.concatenate([x, x], axis=1), "phase": cat(ph, ph), "abslog": cat(al, al), "consts": consts,
        "ids": f("x_txt").reshape(NIT, P).T,
        "table": cat(f("L0_txt_orig_table"), f("L0_txt_new_table")),
        "wq": chunks(f("L0_attn_wq")).reshape(P, -1), "wk": chunks(f("L0_attn_wk")).reshape(P, -1),
        "wv": chunks(wv).reshape(P, -1), "wb": chunks(f("L0_ffn_W_base")).reshape(P, -1),
        "bias": bias, "gate_a": ga.reshape(P, -1), "lora_b": cat(lb, lb),
    }
    arrays = {f"in_{k}": np.ascontiguousarray(v) for k, v in arrays.items()}
    nc = bacc.Bacc("TRN2", target_bir_lowering=False, num_devices=1)
    aps = [nc.dram_tensor(k, v.shape, mb.dt.from_np(v.dtype), kind="ExternalInput").ap() for k, v in arrays.items()]
    out = nc.dram_tensor("out_rows", (NTILE * P, D), mb.dt.float32, kind="ExternalOutput").ap()
    build_kernel(nc, *aps, out)
    rows = run_bass_kernel_spmd(nc, [arrays], core_ids=[0]).results[0]["out_rows"].reshape(NIT, 3, P, D)
    ssm = rows[:, 1:3].reshape(NROW, NCH, D).transpose(1, 0, 2)
    text = rows[:, 0].reshape(NCH, 32, D)
    return np.concatenate([ssm, text], axis=1)
```
